# Optimizing a Trainium2 kernel written in Bass

```python
import numpy as np
import jax
import jax.numpy as jnp

def _softmax(x, axis=-1):
    return jax.nn.softmax(x, axis=axis)

def _gelu(x):
    return jax.nn.gelu(x, approximate=True)

def _silu(x):
    return jax.nn.silu(x)

def _sigmoid(x):
    return jax.nn.sigmoid(x)

def _layernorm(x, axis=-1, eps=1e-05):
    m = jnp.mean(x, axis=axis, keepdims=True)
    v = jnp.var(x, axis=axis, keepdims=True)
    return (x - m) / jnp.sqrt(v + eps)

def _scatter_add(tgt, idx, src, axis=0):
    return tgt.at[idx].add(src)

def _segment_sum(src, seg, n):
    return jax.ops.segment_sum(src, seg, n)
kernel_name = 'mk_lm_tower_d1_tok_ids768_r4_87e100'

def setup_inputs(seed: int=0):
    np.random.seed(seed)
    _w = jnp.asarray

    def _rec_inputs():
        import jax
        import jax.numpy as jnp
        _rk = jax.random.key(seed)
        x = jax.random.randint(jax.random.fold_in(_rk, 1), (8, 1024), 0, 31999, jnp.int32)
        mask_BS_i2_0 = jnp.where(jnp.ones((8, 1024), dtype=bool), 2, 0).astype(jnp.int32)
        return (x, mask_BS_i2_0)
    x, mask_BS_i2_0 = _rec_inputs()

    def _L0_tok_setup():
        import jax, jax.numpy as jnp
        import numpy as np
        VOCAB = 8000
        DIM = 192
        BATCH = 8
        SEQ = 512

        def _sinusoidal_pos(seq_len, dim):
            pos = jnp.arange(seq_len, dtype=jnp.float32)[:, None]
            ids = jnp.arange(dim, dtype=jnp.float32)[None, :]
            even_exp = jnp.floor(ids / 2.0) * 2.0 / dim
            angle = pos / jnp.power(10000.0, even_exp)
            return jnp.where(jnp.arange(dim) % 2 == 0, jnp.sin(angle), jnp.cos(angle))
        key = jax.random.key(seed)
        k1, k2, k3, k4 = jax.random.split(key, 4)
        input_tensor = jax.random.randint(k1, (BATCH, SEQ), 0, VOCAB)
        segment_label = jax.random.randint(k2, (BATCH, SEQ), 0, 3)
        token_table = jax.random.normal(k3, (VOCAB, DIM), dtype=jnp.float32) * 0.02
        segm_table = jax.random.normal(k4, (3, DIM), dtype=jnp.float32) * 0.02
        token_table = token_table.at[0].set(0.0)
        segm_table = segm_table.at[0].set(0.0)
        return {'input_tensor': input_tensor, 'segment_label': segment_label, 'token_table': token_table, 'segm_table': segm_table}
    _L0_tok_all = _L0_tok_setup()
    _L0_tok_in = {k: v for k, v in _L0_tok_all.items() if k in ('token_table', 'segm_table')}
    del _L0_tok_all

    def _L0_attn_setup():
        import jax, jax.numpy as jnp
        import numpy as np
        B, N, C = (8, 256, 192)
        H = 12
        D = C // H
        SCALE = D ** (-0.5)
        EPS = 1e-05

        def _layer_norm(x):
            mean = x.mean(-1, keepdims=True)
            var = ((x - mean) ** 2).mean(-1, keepdims=True)
            return (x - mean) / jnp.sqrt(var + EPS)
        key = jax.random.key(seed)
        k1, k2, k3 = jax.random.split(key, 3)
        x = jax.random.normal(k1, (B, N, C), dtype=jnp.float32)
        qkv_weight = jax.random.normal(k2, (3 * C, C), dtype=jnp.float32) * C ** (-0.5)
        proj_weight = jax.random.normal(k3, (C, C), dtype=jnp.float32) * C ** (-0.5)
        return {'x': x, 'qkv_weight': qkv_weight, 'proj_weight': proj_weight}
    _L0_attn_all = _L0_attn_setup()
    _L0_attn_in = {k: v for k, v in _L0_attn_all.items() if k in ('qkv_weight', 'proj_weight')}
    del _L0_attn_all

    def _L0_ffn_setup():
        import jax, jax.numpy as jnp
        import numpy as np
        QN, QP = (-8, 7)

        def round_pass(x):
            return x + jax.lax.stop_gradient(jnp.round(x) - x)

        def _quant_act(x, alpha_a):
            a = alpha_a.mean()
            return round_pass(jnp.clip(x / a, QN, QP))

        def _quant_w(w, alpha_w):
            return round_pass(jnp.clip(w / alpha_w[:, None], QN, QP))
        key = jax.random.key(seed)
        ks = jax.random.split(key, 9)
        B, S, D, H = (16, 256, 192, 768)

        def unif(k, shape):
            return jax.random.uniform(k, shape, jnp.float32, 0.02, 0.1)
        return {'x0': jax.random.normal(ks[0], (B, S, D), jnp.float32), 'w1': jax.random.normal(ks[1], (H, D), jnp.float32) * 0.02, 'b1': jax.random.normal(ks[2], (H,), jnp.float32) * 0.02, 'alpha_w1': unif(ks[3], (H,)), 'alpha_a1': unif(ks[4], (D,)), 'w2': jax.random.normal(ks[5], (D, H), jnp.float32) * 0.02, 'b2': jax.random.normal(ks[6], (D,), jnp.float32) * 0.02, 'alpha_w2': unif(ks[7], (D,)), 'alpha_a2': unif(ks[8], (H,))}
    _L0_ffn_all = _L0_ffn_setup()
    _L0_ffn_in = {k: v for k, v in _L0_ffn_all.items() if k in ('w1', 'b1', 'alpha_w1', 'alpha_a1', 'w2', 'b2', 'alpha_w2', 'alpha_a2')}
    del _L0_ffn_all
    return {'x': x, 'mask_BS_i2_0': mask_BS_i2_0, 'L0_tok_token_table': _L0_tok_in['token_table'], 'L0_tok_segm_table': _L0_tok_in['segm_table'], 'L0_attn_qkv_weight': _L0_attn_in['qkv_weight'], 'L0_attn_proj_weight': _L0_attn_in['proj_weight'], 'L0_ffn_w1': _L0_ffn_in['w1'], 'L0_ffn_b1': _L0_ffn_in['b1'], 'L0_ffn_alpha_w1': _L0_ffn_in['alpha_w1'], 'L0_ffn_alpha_a1': _L0_ffn_in['alpha_a1'], 'L0_ffn_w2': _L0_ffn_in['w2'], 'L0_ffn_b2': _L0_ffn_in['b2'], 'L0_ffn_alpha_w2': _L0_ffn_in['alpha_w2'], 'L0_ffn_alpha_a2': _L0_ffn_in['alpha_a2']}

def reference(x, mask_BS_i2_0, L0_tok_token_table, L0_tok_segm_table, L0_attn_qkv_weight, L0_attn_proj_weight, L0_ffn_w1, L0_ffn_b1, L0_ffn_alpha_w1, L0_ffn_alpha_a1, L0_ffn_w2, L0_ffn_b2, L0_ffn_alpha_w2, L0_ffn_alpha_a2):
    import jax
    import jax.numpy as jnp

    def _L0_tok_ref(input_tensor, segment_label, token_table, segm_table):
        import jax, jax.numpy as jnp
        import numpy as np
        VOCAB = 8000
        DIM = 192
        BATCH = 8
        SEQ = 512

        def _sinusoidal_pos(seq_len, dim):
            pos = jnp.arange(seq_len, dtype=jnp.float32)[:, None]
            ids = jnp.arange(dim, dtype=jnp.float32)[None, :]
            even_exp = jnp.floor(ids / 2.0) * 2.0 / dim
            angle = pos / jnp.power(10000.0, even_exp)
            return jnp.where(jnp.arange(dim) % 2 == 0, jnp.sin(angle), jnp.cos(angle))
        batch, seq = input_tensor.shape
        pos = _sinusoidal_pos(seq, token_table.shape[1])
        tokens_embed = token_table[input_tensor]
        segments_embed = segm_table[segment_label]
        return segments_embed + pos[None, :, :] + tokens_embed

    def _L0_attn_ref(x, qkv_weight, proj_weight):
        import jax, jax.numpy as jnp
        import numpy as np
        B, N, C = (8, 256, 192)
        H = 12
        D = C // H
        SCALE = D ** (-0.5)
        EPS = 1e-05

        def _layer_norm(x):
            mean = x.mean(-1, keepdims=True)
            var = ((x - mean) ** 2).mean(-1, keepdims=True)
            return (x - mean) / jnp.sqrt(var + EPS)
        Bx, Nx, Cx = x.shape
        qkv = x @ qkv_weight.T
        qkv = qkv.reshape(Bx, Nx, 3, H, D).transpose(2, 0, 3, 1, 4)
        q, k, v = (qkv[0], qkv[1], qkv[2])
        q = _layer_norm(q) * SCALE
        k = _layer_norm(k)
        attn = jnp.einsum('bhnd,bhmd->bhnm', q, k)
        attn = jax.nn.softmax(attn, axis=-1)
        out = jnp.einsum('bhnm,bhmd->bhnd', attn, v)
        out = out.transpose(0, 2, 1, 3).reshape(Bx, Nx, Cx)
        return out @ proj_weight.T

    def _L0_ffn_ref(x0, w1, b1, alpha_w1, alpha_a1, w2, b2, alpha_w2, alpha_a2):
        import jax, jax.numpy as jnp
        import numpy as np
        QN, QP = (-8, 7)

        def round_pass(x):
            return x + jax.lax.stop_gradient(jnp.round(x) - x)

        def _quant_act(x, alpha_a):
            a = alpha_a.mean()
            return round_pass(jnp.clip(x / a, QN, QP))

        def _quant_w(w, alpha_w):
            return round_pass(jnp.clip(w / alpha_w[:, None], QN, QP))
        xq = _quant_act(x0, alpha_a1)
        wq1 = _quant_w(w1, alpha_w1)
        x1 = jnp.einsum('bsd,hd->bsh', xq, wq1)
        x1 = x1 * alpha_w1 * alpha_a1.mean() + b1
        x1 = jax.nn.gelu(x1, approximate=False)
        x1 = jnp.clip(x1, -10.0, 10.0)
        hq = _quant_act(x1, alpha_a2)
        wq2 = _quant_w(w2, alpha_w2)
        x2 = jnp.einsum('bsh,dh->bsd', hq, wq2)
        x2 = x2 * alpha_w2 * alpha_a2.mean() + b2
        return x2
    h = _L0_tok_ref(x, mask_BS_i2_0, L0_tok_token_table, L0_tok_segm_table)
    h = h + _L0_attn_ref(_layernorm(h, axis=-1), L0_attn_qkv_weight, L0_attn_proj_weight)
    h = h + _L0_ffn_ref(_layernorm(h, axis=-1), L0_ffn_w1, L0_ffn_b1, L0_ffn_alpha_w1, L0_ffn_alpha_a1, L0_ffn_w2, L0_ffn_b2, L0_ffn_alpha_w2, L0_ffn_alpha_a2)
    return h

_drawn_inputs = setup_inputs


def setup_inputs(seed=0):
    import zlib

    import numpy as np

    out = dict(_drawn_inputs(seed))
    spreads = {}
    factors = {'L0_ffn_b1': 5.012,
     'L0_ffn_alpha_a2': 64.0,
     'L0_ffn_alpha_w1': 2.802,
     'L0_ffn_alpha_w2': 3.183}
    for name, (base, spread) in spreads.items():
        noise = np.random.default_rng([zlib.crc32(name.encode()), seed]).standard_normal(out[name].shape)
        drawn = base * np.exp(spread * noise) if base else spread * noise
        out[name] = jnp.asarray(drawn.astype(out[name].dtype))
    for name, factor in factors.items():
        out[name] = (out[name] * factor).astype(out[name].dtype)
    return out
```

```python
from contextlib import ExitStack

import concourse.bass as bass
from concourse import mybir

F32 = mybir.dt.float32
F16 = mybir.dt.float16
BF16 = mybir.dt.bfloat16
I32 = mybir.dt.int32
ALU = mybir.AluOpType
ACT = mybir.ActivationFunctionType
X = mybir.AxisListType.X

P = 128
B, SEQ = 8, 1024
C = 192
H, D = 12, 16
HID = 768
TB = SEQ // P
TH = TB // 2
NQ = TH * P
HALVES = 2 * B
KC = C // 2
HB = HID // P
WB = 3 * C // KC
GH = 4
HG = H // GH
VE = D + 1
VW = H * VE + 2 * D - VE
GROUPS = 2 * H
UNITS = HG * TB
EPS = 1e-5
QN, QP = -8.0, 7.0
GELU_CLIP = 10.0
ROUND = 1.5 * 2.0 ** 23
MAGIC = float(0x5F3759DF)
QK_SCALE = 64.0
SCORE_SCALE = D ** -0.5 / QK_SCALE ** 2

ORDER = ("Y0 Y1 P0 Y2 Y3 A0 F0 A1 F1 A2 F2 A3 F3 B0 C0 B1 C1 r0 B2 C2 r1 B3 r2 C3 r3 R0 G0 G1 n0 G2 G3 n1 "
         "H0 H1 D0 H2 H3 L0 E0 D1 E1 n2 D2 E2 I0 I1 n3 D3 I2 I3 E3 X0 X1 X2 X3 X4 X5")
WORK = [(w[0], int(w[1])) for w in ORDER.split()]
JOBS = [w for w in WORK if w[0] in "ABCDEFGHIXY"]
BANKS = 3
X_UNIT = 21
LAG = {**dict.fromkeys("ABCDE", 2), **dict.fromkeys("FGHIX", -1), "Y": -2}
PER_HALF = {**dict.fromkeys("ABCDEFGHIY", TH), "X": HB}
EVACS = {"B": 2, "E": 2}


def job_half(kind, s):
    return s + LAG[kind]


def job_runs(kind, s0):
    return 0 <= job_half(kind, s0) < HALVES


def unit_work():
    units = [[] for _ in range(UNITS)]
    n = 0
    for kind, t in WORK:
        if kind == "X":
            units[X_UNIT].append((kind, t))
            continue
        units[max(n - 1, 0) // 2 if kind in "rRnLP" else n // 2].append((kind, t))
        n += kind not in "rRnLP"
    assert n <= 2 * X_UNIT
    return units


UNIT_WORK = unit_work()


def slots(u):
    work = UNIT_WORK[u]
    if u == X_UNIT:
        return work[:BANKS], work[BANKS:]
    first = [i for i, w in enumerate(work) if w in JOBS]
    cut = first[1] if len(first) > 1 else len(work)
    return work[:cut], work[cut:]


def bank_of(job):
    return JOBS.index(job) % BANKS


def job_before(job, s0):
    at = JOBS.index(job)
    for back in (0, 1):
        for other in reversed(JOBS[:at] if back == 0 else JOBS):
            if bank_of(other) == bank_of(job) and job_runs(other[0], s0 - back):
                return other, back
    return None


def layer(nc, x_tok, x_seg, tok_table, seg_table, w_qkv, w_proj, w1, b1, aw1, aa1, w2, b2, aw2, aa2,
          pos, out):
    ctx = ExitStack()
    with ctx:
        def sb(name, shape, dt=F32):
            return ctx.enter_context(nc.sbuf_tensor(name, shape, dt))

        def sem(name):
            return ctx.enter_context(nc.semaphore(name))

        h_all = sb("h_all", [P, B * TB * C])
        probs = sb("probs", [P, 2, GH, NQ])
        qT = sb("qT", [P, 2, H // 2, SEQ], F16)
        kA = sb("kA", [P, 2, H // 2, SEQ], F16)
        kB = sb("kB", [P, 2, H // 2, SEQ], F16)
        v_sb = sb("v_sb", [P, 2, TB, VW])
        hn = sb("hn", [P, TH, C])
        hT = sb("hT", [KC, TH, 2, P])
        stack = sb("stack", [P, 2, 2, H, 4, D], F16)
        o_sb = sb("o_sb", [P, HG, NQ])
        xq = sb("xq", [P, TH, C], BF16)
        xqT = sb("xqT", [KC, 2, NQ], BF16)
        gelu = sb("gelu", [P, HB, NQ])
        hq = sb("hq", [P, HB, NQ], BF16)
        o_nat, oT = hn, hT
        gelu_f = gelu[:].rearrange("p j n -> p (j n)")
        xf = gelu_f[:, 0:TH * C].rearrange("p (t c) -> p t c", c=C)
        qkn = gelu_f[:, 0:2 * C]
        y_sb = gelu_f[:, TH * C:2 * TH * C].rearrange("p (t c) -> p t c", c=C)
        sq = gelu_f[:, 2 * TH * C:4 * TH * C].rearrange("p (t c) -> p t c", c=2 * C)
        qk = hq[:].rearrange("p j n -> p (j n)").bitcast(F32).rearrange("p (t c) -> p t c", c=2 * C)
        st = sb("st", [P, TH, 6])
        mv = sb("mv", [P, TH, 2])
        va, ra, wa = sb("va", [P, TH]), sb("ra", [P, TH]), sb("wa", [P, TH])
        vq, rq, wq_ = (sb(n, [P, TH, GROUPS]) for n in ("vq", "rq", "wq_"))
        rsum = sb("rsum", [P, H])
        gate_sb = sb("gate_sb", [P, 1])
        wT = sb("wT", [KC, 2, 3 * C])
        wmean = sb("wmean", [KC, 2, GROUPS])
        wpT = sb("wpT", [KC, 2, C])
        w1T = sb("w1T", [KC, 2, HID], BF16)
        w2T = sb("w2T", [P, HB, C], BF16)
        a1, ia1, a2, ia2 = (sb(n, [P, 1]) for n in ("a1", "ia1", "a2", "ia2"))
        bound, qlo, qhi = (sb(n, [P, 1]) for n in ("bound", "qlo", "qhi"))
        aw1_sb, iaw1, s1_sb, b1_sb = (sb(n, [P, HB]) for n in ("aw1_sb", "iaw1", "s1_sb", "b1_sb"))
        aw2c, iaw2 = sb("aw2c", [KC, 2]), sb("iaw2", [KC, 2])
        s2_row, b2_row = sb("s2_row", [P, C]), sb("b2_row", [P, C])
        ident = sb("ident", [P, P])
        ident_h = sb("ident_h", [P, P], F16)
        ident_b = sb("ident_b", [P, P], BF16)
        idx_in = sb("idx_in", [P, 2, B, TB], I32)
        idx_f = sb("idx_f", [P, 2, B, TB])
        idx = sb("idx", [P, 2, B * TB], I32)
        start_f = probs[:].rearrange("p a g n -> p (a g n)")
        hq_f = hq[:].rearrange("p j n -> p (j n)")
        wq_nat = start_f[0:KC, 0:WB * C].rearrange("p (r c) -> p r c", c=C)
        wp_nat = start_f[0:KC, WB * C:(WB + 2) * C].rearrange("p (r c) -> p r c", c=C)
        aa1_in = start_f[:, (WB + 2) * C:(WB + 3) * C]
        aa2_in = start_f[:, (WB + 3) * C:(WB + 3) * C + HID]
        w1_nat = gelu_f[:, 0:HB * C].rearrange("p (j c) -> p j c", c=C)
        w2_nat = gelu_f[0:KC, HB * C:HB * C + 2 * HID].rearrange("p (r h) -> p r h", h=HID)
        w1_q = hq_f[:, 0:HB * C].rearrange("p (j c) -> p j c", c=C)
        w2_q = hq_f[0:KC, HB * C:HB * C + 2 * HID].rearrange("p (r h) -> p r h", h=HID)

        ps_s = ctx.enter_context(nc.psum_tensor("ps_s", [P, GH, NQ], F32))
        ps_o = ctx.enter_context(nc.psum_tensor("ps_o", [P, NQ], F32))
        ps_j = ctx.enter_context(nc.psum_tensor("ps_j", [P, BANKS, 512], F32))

        idx_loaded, w_loaded, aw_loaded = sem("idx_loaded"), sem("w_loaded"), sem("aw_loaded")
        pos_loaded, seg_added, tok_added = sem("pos_loaded"), sem("seg_added"), sem("tok_added")
        idx_ready, ident_ready, filled = sem("idx_ready"), sem("ident_ready"), sem("filled")
        pool_step, dve_step = sem("pool_step"), sem("dve_step")
        weights_q, weights_mm, weights_ready = sem("weights_q"), sem("weights_mm"), sem("weights_ready")
        hn_ready, stack_ready, xq_ready, hq_ready = (
            sem(n) for n in ("hn_ready", "stack_ready", "xq_ready", "hq_ready"))
        scores_mm, exp_done, heads_mm, heads_out = (
            sem(n) for n in ("scores_mm", "exp_done", "heads_mm", "heads_out"))
        out_ready, stored = sem("out_ready"), sem("stored")
        job_mm = {k: sem(f"{k}_mm") for k in PER_HALF}
        job_out = {k: sem(f"{k}_out") for k in PER_HALF}

        def nth(half, t, per):
            return half * per + (t + 1)

        def out_count(job, half):
            kind, t = job
            return (half * PER_HALF[kind] + (t + 1)) * EVACS.get(kind, 1)

        def h_tile(half, t):
            return h_all[:, bass.ds(half * (TH * C) + t * C, C)]

        def bank(job):
            return ps_j[:, bank_of(job), :]

        def bank16(job, dt):
            return ps_j[:, bank_of(job), :].bitcast(dt)

        def attends(s0):
            return 0 <= s0 < HALVES

        def halfsteps(eng, one):
            for s in range(-2, 2):
                one(s, s, s // 2)
            with eng.Fori(0, (B - 2) // 2) as turn:
                for k in range(4):
                    one(2 + k, turn * 4 + (2 + k), turn * 2 + (1 + k // 2))
            for s in range(HALVES - 2, HALVES + 2):
                one(s, s, s // 2)

        block = ctx.enter_context(nc.Block())

        @block.sync
        def _(sp):
            sp.dma_start(idx_in[:, 0], x_tok.rearrange("b (p j) -> p b j", j=TB)).then_inc(idx_loaded, 16)
            sp.dma_start(idx_in[:, 1], x_seg.rearrange("b (p j) -> p b j", j=TB)).then_inc(idx_loaded, 16)
            pos_v = pos.rearrange("(p j) c -> p (j c)", j=TB)

            def load_pos(b):
                sp.dma_start(h_all[:, b * TB * C:(b + 1) * TB * C], pos_v).then_inc(pos_loaded, 16)
                sp.wait_ge(pos_loaded, 16 * (b + 1))

            load_pos(0)
            sp.dma_start(wq_nat, w_qkv.rearrange("(r p) c -> p r c", p=KC)).then_inc(w_loaded, 16)
            sp.dma_start(wp_nat, w_proj.rearrange("(r p) c -> p r c", p=KC)).then_inc(w_loaded, 16)
            sp.dma_start(w1_nat, w1.rearrange("(p j) c -> p j c", j=HB)).then_inc(w_loaded, 16)
            sp.dma_start(w2_nat, w2.rearrange("(p r) h -> p r h", r=2)).then_inc(w_loaded, 16)
            for b in range(1, B):
                load_pos(b)

            def one(s0, s, b):
                if not job_runs("Y", s0):
                    return
                y = job_half("Y", s)
                sp.wait_ge(out_ready, nth(y, 0, 1))
                sp.dma_start(out_rows[:, bass.ds(b - 1, 1), s0 % 2 * TH * C:(s0 % 2 + 1) * TH * C],
                             h_all[:, bass.ds(y * (TH * C), TH * C)]).then_inc(stored, 16)

            out_rows = out.rearrange("b (p j) c -> p b (j c)", j=TB)
            halfsteps(sp, one)
            sp.wait_ge(stored, 16 * HALVES)

        @block.gpsimd
        def _(pool):
            def gather(table, which, b, done):
                for j in range(TB):
                    t = b * TB + j
                    nc.gpsimd.indirect_dma_start(
                        out=h_all[:, t * C:(t + 1) * C], out_offset=None, in_=table,
                        in_offset=bass.IndirectOffsetOnAxis(ap=idx[:, which, t:t + 1], axis=0),
                        compute_op=ALU.add).then_inc(done, 16)

            for m in (ident, ident_h, ident_b):
                nc.gpsimd.memset(m[:], 0.0).then_inc(pool_step, 1)
            for n, m in enumerate((ident, ident_h, ident_b)):
                pool.wait_ge(pool_step, n + 1)
                nc.gpsimd.affine_select(out=m[:], in_=m[:], compare_op=ALU.not_equal, fill=1.0, base=0,
                                        pattern=[[-1, P]], channel_multiplier=1).then_inc(ident_ready, 1)
            pool.wait_ge(idx_ready, 1)
            for b in range(B):
                pool.wait_ge(pos_loaded, 16 * (b + 1))
                gather(seg_table, 1, b, seg_added)
                pool.wait_ge(seg_added, 16 * TB * (b + 1))
                if b:
                    pool.wait_ge(tok_added, 16 * TB * b)
                gather(tok_table, 0, b, tok_added)
                if b < 2:
                    if b == 0:
                        pool.wait_ge(ident_ready, 3)
                    else:
                        pool.wait_ge(filled, 3 * b)
                    nc.gpsimd.memset(kA[P // 2:P, b].bitcast(F32), 0.0).then_inc(filled, 1)
                    pool.wait_ge(filled, 3 * b + 1)
                    nc.gpsimd.memset(kB[0:P // 2, b].bitcast(F32), 0.0).then_inc(filled, 1)
                    pool.wait_ge(filled, 3 * b + 2)
                    nc.gpsimd.memset(v_sb[:, b], 1.0).then_inc(filled, 1)

            def one(s0, s, b):
                if not job_runs("Y", s0):
                    return
                y = job_half("Y", s)
                pool.wait_ge(job_out["Y"], nth(y, TH - 1, TH))
                nc.gpsimd.tensor_tensor(y_sb, y_sb, b2_row[:].unsqueeze(1).broadcast_to([P, TH, C]),
                                        ALU.add).then_inc(pool_step, 1)
                pool.wait_ge(pool_step, y + 4)
                hv = h_all[:, bass.ds(y * (TH * C), TH * C)]
                nc.gpsimd.tensor_tensor(hv, hv, gelu_f[:, TH * C:2 * TH * C],
                                        ALU.add).then_inc(out_ready, 1)

            halfsteps(pool, one)

        @block.scalar
        def _(act):
            act.dma_start(aa1_in, aa1.unsqueeze(0).broadcast_to([P, C])).then_inc(aw_loaded, 16)
            act.dma_start(aa2_in, aa2.unsqueeze(0).broadcast_to([P, HID])).then_inc(aw_loaded, 16)
            act.dma_start(aw1_sb[:], aw1.rearrange("(p j) -> p j", j=HB)).then_inc(aw_loaded, 16)
            act.dma_start(b1_sb[:], b1.rearrange("(p j) -> p j", j=HB)).then_inc(aw_loaded, 16)
            act.dma_start(aw2c[:], aw2.rearrange("(p r) -> p r", r=2)).then_inc(aw_loaded, 16)
            act.dma_start(s2_row[:], aw2.unsqueeze(0).broadcast_to([P, C])).then_inc(aw_loaded, 16)
            act.dma_start(b2_row[:], b2.unsqueeze(0).broadcast_to([P, C])).then_inc(aw_loaded, 16)
            act.wait_ge(weights_ready, 1)

            def qk_out(s0, s, t):
                half = job_half("B", s)
                act.wait_ge(job_mm["B"], nth(half, t, TH))
                if job_half("B", s0) >= 1:
                    act.wait_ge(stack_ready, nth(half - 1, t, TH))
                if t == 0 and job_runs("X", s0 - 1):
                    act.wait_ge(hq_ready, nth(job_half("X", s - 1), HB - 1, HB))
                src = bank(("B", t))[:, 0:2 * C]
                nc.scalar.activation(qk[:, t], src, ACT.Copy).then_inc(job_out["B"], 1)
                nc.scalar.activation(sq[:, t], src, ACT.Square).then_inc(job_out["B"], 1)

            def v_out(s0, s, t):
                p0 = job_half("C", s0)
                act.wait_ge(job_mm["C"], nth(job_half("C", s), t, TH))
                nc.scalar.activation(v_sb[:, p0 // 2 % 2, p0 % 2 * TH + t, 0:H * VE].rearrange("p (h e) -> p h e", e=VE)[:, :, 0:D],
                                     bank(("C", t))[:, 0:C].rearrange("p (h d) -> p h d", d=D),
                                     ACT.Copy).then_inc(job_out["C"], 1)

            def gelu_out(s0, s, j):
                half = job_half("X", s)
                act.wait_ge(job_mm["X"], nth(half, j, HB))
                if j == 0 and job_runs("Y", s0):
                    act.wait_ge(out_ready, nth(job_half("Y", s), 0, 1))
                nc.scalar.activation(gelu[:, j], bank(("X", j)), ACT.Gelu, bias=b1_sb[:, j:j + 1],
                                     scale=s1_sb[:, j:j + 1]).then_inc(job_out["X"], 1)

            def exps(s0, s, u, pair):
                act.wait_ge(scores_mm, 2 * UNITS * s + (2 * u + pair + 1))
                nc.scalar.activation(probs[:, u % 2, 2 * pair:2 * pair + 2], ps_s[:, 2 * pair:2 * pair + 2],
                                     ACT.Exp, scale=SCORE_SCALE).then_inc(exp_done, 1)

            def one(s0, s, b):
                for u in range(UNITS):
                    work = slots(u)
                    if u == X_UNIT and job_runs("X", s0):
                        for j in range(HB):
                            gelu_out(s0, s, j)
                    for pair in range(2):
                        if attends(s0):
                            exps(s0, s, u, pair)
                        for kind, t in work[pair]:
                            if kind == "B" and job_runs("B", s0):
                                qk_out(s0, s, t)
                            if kind == "C" and job_runs("C", s0):
                                v_out(s0, s, t)

            halfsteps(act, one)

        @block.vector
        def _(dve):
            steps = {"done": 0, "turns": 0}

            def link(ins):
                steps["done"] += 1
                ins.then_inc(dve_step, 1)
                dve.wait_ge(dve_step, steps["turns"] + steps["done"])

            ts = nc.vector.tensor_scalar
            tt = nc.vector.tensor_tensor
            stt = nc.vector.scalar_tensor_tensor

            def rsqrt(y, v, w):
                link(ts(w.bitcast(I32), v.bitcast(I32), 1, None, ALU.logical_shift_right))
                link(ts(y.bitcast(I32), w.bitcast(I32), -1.0, MAGIC, ALU.mult, ALU.add))
                for _ in range(3):
                    link(stt(out=w, in0=y, scalar=-0.5, in1=y, op0=ALU.mult, op1=ALU.mult))
                    link(tt(w, w, v, ALU.mult))
                    link(stt(out=y, in0=w, scalar=1.5, in1=y, op0=ALU.add, op1=ALU.mult))

            def gate():
                nc.vector.memset(gate_sb[:], 0.0)

            def norm_stats(half):
                gate()
                for t in range(TH):
                    last = nc.vector.bn_stats(st[:, t], h_tile(half, t))
                link(last)
                gate()
                for t in range(TH):
                    last = nc.vector.bn_aggr(mv[:, t], st[:, t])
                link(last)
                link(ts(va[:], mv[:, :, 1], EPS, None, ALU.add))
                rsqrt(ra[:], va[:], wa[:])

            def first_norm(p0, p):
                if not 0 <= p0 < HALVES:
                    return
                b = p0 // 2
                dve.wait_ge(tok_added, (p - p0 % 2 + 2) * (TB * 8))
                norm_stats(p)
                if p0:
                    dve.wait_ge(job_mm["A"], nth(p - 1, TH - 1, TH))
                for t in range(TH):
                    ts(hn[:, t], h_tile(p, t), mv[:, t, 0:1], ra[:, t:t + 1],
                       ALU.subtract, ALU.mult).then_inc(hn_ready, 1)

            def quantise(dst, src, tmp, lo, hi):
                link(ts(tmp, src, lo, hi, ALU.max, ALU.min))
                return ts(dst, tmp, ROUND, -ROUND, ALU.add, ALU.add)

            def copy_out(job, half, dst, src):
                dve.wait_ge(job_mm[job[0]], nth(half, job[1], PER_HALF[job[0]]))
                nc.vector.tensor_copy(dst, src).then_inc(job_out[job[0]], 1)

            def squares_sum(s0, s, t):
                half = job_half("B", s)
                dve.wait_ge(job_out["B"], out_count(("B", t), half))
                link(nc.vector.tensor_reduce(vq[:, t], sq[:, t].rearrange("p (g d) -> p g d", d=D), X, ALU.add))

            def qk_rsqrt():
                link(ts(vq[:], vq[:], 1.0 / (D * QK_SCALE ** 2), EPS / QK_SCALE ** 2, ALU.mult, ALU.add))
                rsqrt(rq[:], vq[:], wq_[:])

            def split_qk(s0, s, t):
                half, h0 = job_half("D", s), job_half("D", s0)
                g = lambda a: a.rearrange("p (g d) -> p g d", d=D)
                if TH * h0 + t:
                    dve.wait_ge(stack_ready, half * TH + t)
                if job_runs("I", s0) and WORK.index(("n", t)) > WORK.index(("L", 0)):
                    dve.wait_ge(xq_ready, nth(job_half("I", s), 0, 1))
                link(tt(g(qkn), g(qk[:, t]), rq[:, t].unsqueeze(2).broadcast_to([P, GROUPS, D]), ALU.mult))
                if TH * h0 + t >= 2:
                    dve.wait_ge(job_mm["E"], half * TH + (t - 1))
                for n, (hi, lo) in enumerate((((0, 2, 1), (2, 4, 1)), ((0, 4, 2), (1, 4, 2)))):
                    src = qkn[:, n * C:(n + 1) * C].rearrange("p (h d) -> p h d", d=D)
                    src = src.unsqueeze(2).broadcast_to([P, H, 2, D])
                    part = stack[:, t % 2, n]
                    high = part[:, :, hi[0]:hi[1]:hi[2], :]
                    nc.vector.tensor_copy(high, src).then_inc(dve_step, 1)
                    steps["done"] += 1
                dve.wait_ge(dve_step, steps["turns"] + steps["done"])
                for n, (hi, lo) in enumerate((((0, 2, 1), (2, 4, 1)), ((0, 4, 2), (1, 4, 2)))):
                    src = qkn[:, n * C:(n + 1) * C].rearrange("p (h d) -> p h d", d=D)
                    src = src.unsqueeze(2).broadcast_to([P, H, 2, D])
                    part = stack[:, t % 2, n]
                    high = part[:, :, hi[0]:hi[1]:hi[2], :]
                    last = tt(part[:, :, lo[0]:lo[1]:lo[2], :], src, high, ALU.subtract)
                last.then_inc(stack_ready, 1)

            def head_outputs(s0, s, group):
                dve.wait_ge(heads_mm, UNITS * s + TB * (group + 1))
                nc.vector.tensor_copy(o_sb[:, group], ps_o[:]).then_inc(heads_out, 1)

            def second_norm(s0, s):
                half = job_half("I", s)
                norm_stats(half)
                link(ts(ra[:], ra[:], ia1[:], None, ALU.mult))
                for t in range(TH):
                    last = ts(xf[:, t], h_tile(half, t), mv[:, t, 0:1], ra[:, t:t + 1],
                              ALU.subtract, ALU.mult)
                link(last)
                quantise(xq[:], xf, xf, QN, QP).then_inc(xq_ready, 1)

            def job_result(s0, s, kind, t):
                if not job_runs(kind, s0):
                    return
                half, h0 = job_half(kind, s), job_half(kind, s0)
                job = (kind, t)
                ps = bank(job)
                tile = h0 % 2 * TH + t
                par = h0 // 2 % 2
                if kind == "A":
                    copy_out(job, half, hT[:, t], ps[0:KC, 0:2 * P].rearrange("p (k n) -> p k n", k=2))
                if kind == "D":
                    copy_out(job, half, qT[:, par, :, tile * P:(tile + 1) * P],
                             bank16(job, F16)[:, 0:HB * P].rearrange("p (i n) -> p i n", n=P))
                if kind == "E":
                    for lo, dst in ((0, kA), (P // 2, kB)):
                        copy_out(job, half, dst[lo:lo + P // 2, par, :, tile * P:(tile + 1) * P],
                                 bank16(job, F16)[lo:lo + P // 2, 0:HB * P].rearrange("p (i n) -> p i n", n=P))
                if kind == "F":
                    dve.wait_ge(job_mm["F"], nth(half, t, TH))
                    heads = ps[:, 0:H * 2 * D].rearrange("p (h e) -> p h e", e=2 * D)
                    if h0 or t:
                        dve.wait_ge(job_out["F"], half * TH + t)
                    link(nc.vector.reciprocal(rsum[:], heads[:, :, D]))
                    tt(o_nat[:, t].rearrange("p (h d) -> p h d", d=D), heads[:, :, 0:D],
                       rsum[:].unsqueeze(2).broadcast_to([P, H, D]), ALU.mult).then_inc(job_out["F"], 1)
                if kind == "G":
                    copy_out(job, half, oT[:, t], ps[0:KC, 0:2 * P].rearrange("p (k n) -> p k n", k=2))
                if kind == "H":
                    dve.wait_ge(job_mm["H"], nth(half, t, TH))
                    tt(h_tile(half, t), ps[:, 0:C], h_tile(half, t), ALU.add).then_inc(job_out["H"], 1)
                    if t == TH - 1:
                        dve.wait_ge(job_out["H"], nth(half, t, TH))
                if kind == "I":
                    copy_out(job, half, xqT[:, :, t * P:(t + 1) * P],
                             bank16(job, BF16)[0:KC, 0:2 * P].rearrange("p (k n) -> p k n", k=2))
                if kind == "X":
                    dve.wait_ge(job_out["X"], nth(half, t, HB))
                    link(ts(gelu[:, t], gelu[:, t], ia2[:], qlo[:], ALU.mult, ALU.max))
                    link(ts(gelu[:, t], gelu[:, t], qhi[:], ROUND, ALU.min, ALU.add))
                    ts(hq[:, t], gelu[:, t], ROUND, None, ALU.subtract).then_inc(hq_ready, 1)
                if kind == "Y":
                    dve.wait_ge(job_mm["Y"], nth(half, t, TH))
                    if h0 >= 1 and t == 0:
                        dve.wait_ge(out_ready, nth(half - 1, 0, 1))
                    tt(y_sb[:, t], ps[:, 0:C], s2_row[:], ALU.mult).then_inc(job_out["Y"], 1)

            def start():
                dve.wait_ge(idx_loaded, 32)
                for w, rows in ((0, tok_table.shape[0]), (1, seg_table.shape[0])):
                    link(ts(idx_f[:, w], idx_in[:, w], 0.0, float(rows), ALU.is_lt, ALU.mult))
                    link(tt(idx_f[:, w], idx_f[:, w], idx_in[:, w], ALU.add))
                    last = ts(idx[:, w], idx_f[:, w].rearrange("p b j -> p (b j)"), 0.0, float(rows - 1),
                              ALU.max, ALU.min)
                last.then_inc(idx_ready, 1)
                dve.wait_ge(aw_loaded, 16 * 7)
                for a, ia, src, n in ((a1, ia1, aa1_in, C), (a2, ia2, aa2_in, HID)):
                    link(nc.vector.tensor_reduce(a[:], src, X, ALU.add))
                    link(ts(a[:], a[:], 1.0 / n, None, ALU.mult))
                    link(nc.vector.reciprocal(ia[:], a[:]))
                link(ts(bound[:], ia2[:], -GELU_CLIP, None, ALU.mult))
                link(stt(out=bound[:], in0=ia2[:], scalar=GELU_CLIP, in1=bound[:], op0=ALU.mult, op1=ALU.max))
                link(ts(qhi[:], bound[:], QP, None, ALU.min))
                link(ts(qlo[:], bound[:], -1.0, QN, ALU.mult, ALU.max))
                link(ts(s1_sb[:], aw1_sb[:], a1[:], None, ALU.mult))
                link(ts(s2_row[:], s2_row[:], a2[:], None, ALU.mult))
                link(nc.vector.reciprocal(iaw1[:], aw1_sb[:]))
                link(nc.vector.reciprocal(iaw2[:], aw2c[:]))
                dve.wait_ge(w_loaded, 16 * 4)
                for nat, q, ia, n in ((w1_nat, w1_q, iaw1, HB), (w2_nat, w2_q, iaw2, 2)):
                    for j in range(n):
                        last = ts(nat[:, j], nat[:, j], ia[:, j:j + 1], None, ALU.mult)
                    link(last)
                    quantise(q, nat, nat, QN, QP).then_inc(weights_q, 1)
                dve.wait_ge(weights_mm, 1)
                for k in range(2):
                    last = nc.vector.tensor_copy(wT[:, k, 0:2 * C], ps_j[0:KC, k, 0:2 * C])
                last = nc.vector.tensor_copy(wT[:, :, 2 * C:3 * C],
                                             ps_j[0:KC, 2, 0:2 * C].rearrange("p (k c) -> p k c", k=2))
                link(last)
                nc.vector.tensor_copy(wpT[:], ps_o[0:KC, 0:2 * C].rearrange("p (k c) -> p k c", k=2))
                for k in range(2):
                    g = wT[:, k, 0:2 * C].rearrange("p (g d) -> p g d", d=D)
                    link(nc.vector.tensor_reduce(wmean[:, k], g, X, ALU.add))
                    link(ts(wmean[:, k], wmean[:, k], -1.0 / D, None, ALU.mult))
                    link(tt(g, g, wmean[:, k].unsqueeze(2).broadcast_to([KC, GROUPS, D]), ALU.add))
                dve.wait_ge(weights_mm, 2)
                for k in range(2):
                    nc.vector.tensor_copy(w1T[:, k], ps_s[0:KC, k].bitcast(BF16)[:, 0:HID])
                for lo, n in ((0, 4), (4, 2)):
                    for j in range(n):
                        last = nc.vector.tensor_copy(
                            w2T[:, lo + j].rearrange("p (c r) -> p c r", r=2),
                            ps_s[:, 2 + lo // 4].bitcast(BF16)[:, j * C:(j + 1) * C].rearrange("p (r c) -> p c r", r=2))
                link(last)
                dve.wait_ge(filled, 6)
                nc.vector.tensor_copy(a1[:], a1[:]).then_inc(weights_ready, 1)

            def one(s0, s):
                for u in range(UNITS):
                    for n, work in enumerate(slots(u)):
                        if n == 1 and u % TB == 0:
                            if u == 0 and attends(s0 - 1):
                                head_outputs(s0 - 1, s - 1, HG - 1)
                            elif u and attends(s0):
                                head_outputs(s0, s, u // TB - 1)
                        for kind, t in work:
                            if kind == "r" and job_runs("B", s0):
                                squares_sum(s0, s, t)
                            elif kind == "R" and job_runs("B", s0):
                                qk_rsqrt()
                            elif kind == "n" and job_runs("D", s0):
                                split_qk(s0, s, t)
                            elif kind == "L" and job_runs("I", s0):
                                second_norm(s0, s)
                            elif kind == "P":
                                first_norm(s0 + 2, s + 2)
                            elif kind in job_out:
                                job_result(s0, s, kind, t)

            start()
            for s in range(-2, 2):
                one(s, s)
            before = steps["done"]
            with dve.Fori(0, (B - 2) // 2) as turn:
                steps["turns"] = turn * LINKS_PER_TURN
                for k in range(4):
                    one(2 + k, turn * 4 + (2 + k))
            assert steps["done"] - before == LINKS_PER_TURN, steps["done"] - before
            steps["turns"] = ((B - 2) // 2 - 1) * LINKS_PER_TURN
            for s in range(HALVES - 2, HALVES + 2):
                one(s, s)

        @block.tensor
        def _(pe):
            mm = nc.tensor.matmul

            def start():
                pe.wait_ge(ident_ready, 3)
                pe.wait_ge(w_loaded, 16 * 4)
                for k in range(2):
                    cols = slice(k * KC, (k + 1) * KC)
                    for r in range(4):
                        nc.tensor.transpose(ps_j[0:KC, k, r * KC:(r + 1) * KC], wq_nat[:, r, cols], ident[0:KC, 0:KC])
                    for r in range(2):
                        nc.tensor.transpose(ps_j[0:KC, 2, k * C + r * KC:k * C + (r + 1) * KC],
                                            wq_nat[:, 4 + r, cols], ident[0:KC, 0:KC])
                    for r in range(2):
                        last = nc.tensor.transpose(ps_o[0:KC, k * C + r * KC:k * C + (r + 1) * KC],
                                                   wp_nat[:, r, cols], ident[0:KC, 0:KC])
                last.then_inc(weights_mm, 1)
                pe.wait_ge(weights_q, 2)
                for k in range(2):
                    for j in range(HB):
                        nc.tensor.transpose(ps_s[0:KC, k].bitcast(BF16)[:, j * P:(j + 1) * P],
                                            w1_q[:, j, k * KC:(k + 1) * KC], ident_b[:])
                for j in range(HB):
                    for r in range(2):
                        at = j % 4 * C + r * KC
                        last = nc.tensor.transpose(ps_s[:, 2 + j // 4].bitcast(BF16)[:, at:at + KC],
                                                   w2_q[:, r, j::HB], ident_b[0:KC, 0:KC])
                last.then_inc(weights_mm, 1)
                pe.wait_ge(weights_ready, 1)

            def scores(s0, s, u):
                par, nh = s0 // 2 % 2, s0 % 2
                group, m = divmod(u, TB)
                if u == 0 and nh == 0:
                    pe.wait_ge(job_out["D"], (s + 2) * TH)
                    pe.wait_ge(job_out["E"], (s + 2) * TH * 2)
                for j in range(GH):
                    if j % 2 == 0 and (u or attends(s0 - 1)):
                        pe.wait_ge(exp_done, 2 * UNITS * s + (2 * u - 1 + j // 2))
                    head = GH * group + j
                    k = kA if head % 2 == 0 else kB
                    last = mm(ps_s[:, j], k[:, par, head // 2, m * P:(m + 1) * P],
                              qT[:, par, head // 2, nh * NQ:(nh + 1) * NQ], start=True, stop=True)
                    if j % 2:
                        last.then_inc(scores_mm, 1)

            def heads(s0, s, u):
                par = s0 // 2 % 2
                group, m = divmod(u, TB)
                if u == 0 and s0 % 2 == 0:
                    pe.wait_ge(job_out["C"], (s + 2) * TH)
                if m == 0 and (group or attends(s0 - 1)):
                    pe.wait_ge(heads_out, HG * s + group)
                pe.wait_ge(exp_done, 2 * UNITS * s + (2 * u + 2))
                for j in range(GH):
                    last = mm(ps_o[32 * j:32 * j + 2 * D, :], v_sb[:, par, m, (GH * group + j) * VE:(GH * group + j) * VE + 2 * D],
                              probs[:, u % 2, j], start=(m == 0), stop=(m == TB - 1))
                last.then_inc(heads_mm, 1)

            def job(s0, s, kind, t):
                if not job_runs(kind, s0):
                    return
                half, h0 = job_half(kind, s), job_half(kind, s0)
                prior = job_before((kind, t), s0)
                if prior:
                    (pk, pt), back = prior
                    pe.wait_ge(job_out[pk], out_count((pk, pt), job_half(pk, s - back)))
                ps = bank((kind, t))
                if kind == "A":
                    pe.wait_ge(hn_ready, nth(half, t, TH))
                    for k in range(2):
                        last = nc.tensor.transpose(ps[0:KC, k * P:(k + 1) * P], hn[:, t, k * KC:(k + 1) * KC], ident[:])
                if kind == "B":
                    pe.wait_ge(job_out["A"], nth(half, t, TH))
                if kind in "BC":
                    lo, hi = (0, 2 * C) if kind == "B" else (2 * C, 3 * C)
                    for k in range(2):
                        last = mm(ps[:, 0:hi - lo], hT[:, t, k], wT[:, k, lo:hi], start=(k == 0), stop=(k == 1))
                if kind in "DE":
                    pe.wait_ge(stack_ready, nth(half, t, TH))
                    for i in range(H // 2):
                        src = stack[:, t % 2, "DE".index(kind), 2 * i:2 * i + 2].rearrange("p h a d -> p (h a d)")
                        last = nc.tensor.transpose(bank16((kind, t), F16)[:, i * P:(i + 1) * P], src, ident_h[:])
                if kind == "F":
                    if t == 0:
                        pe.wait_ge(heads_out, nth(half, HG - 1, HG))
                    for g in range(HG):
                        last = nc.tensor.transpose(ps[:, g * P:(g + 1) * P], o_sb[:, g, t * P:(t + 1) * P], ident[:])
                if kind == "G":
                    pe.wait_ge(job_out["F"], nth(half, t, TH))
                    for k in range(2):
                        last = nc.tensor.transpose(ps[0:KC, k * P:(k + 1) * P], o_nat[:, t, k * KC:(k + 1) * KC], ident[:])
                if kind == "H":
                    pe.wait_ge(job_out["G"], nth(half, t, TH))
                    for k in range(2):
                        last = mm(ps[:, 0:C], oT[:, t, k], wpT[:, k], start=(k == 0), stop=(k == 1))
                if kind == "I":
                    if t == 0:
                        pe.wait_ge(xq_ready, nth(half, 0, 1))
                    for k in range(2):
                        last = nc.tensor.transpose(bank16((kind, t), BF16)[0:KC, k * P:(k + 1) * P],
                                                   xq[:, t, k * KC:(k + 1) * KC], ident_b[:])
                if kind == "X":
                    if t == 0:
                        pe.wait_ge(job_out["I"], nth(half, TH - 1, TH))
                    for k in range(2):
                        last = mm(ps, w1T[:, k, t * P:(t + 1) * P], xqT[:, k], start=(k == 0), stop=(k == 1))
                if kind == "Y":
                    if t == 0:
                        pe.wait_ge(hq_ready, nth(half, HB - 1, HB))
                    for j in range(HB):
                        last = mm(ps[:, 0:C], hq[:, j, t * P:(t + 1) * P], w2T[:, j], start=(j == 0), stop=(j == HB - 1))
                last.then_inc(job_mm[kind], 1)

            def one(s0, s, b):
                for u in range(UNITS):
                    first, second = slots(u)
                    if u == X_UNIT:
                        for kind, t in first:
                            job(s0, s, kind, t)
                        first = []
                    if attends(s0):
                        scores(s0, s, u)
                    for kind, t in first:
                        if kind in job_mm:
                            job(s0, s, kind, t)
                    if u and attends(s0):
                        heads(s0, s, u - 1)
                    elif not u and attends(s0 - 1):
                        heads(s0 - 1, s - 1, UNITS - 1)
                    for kind, t in second:
                        if kind in job_mm:
                            job(s0, s, kind, t)

            start()
            halfsteps(pe, one)


LINKS_PER_TURN = 4 * 75


_INS = ['x', 'mask_BS_i2_0', 'L0_tok_token_table', 'L0_tok_segm_table', 'L0_attn_qkv_weight',
        'L0_attn_proj_weight', 'L0_ffn_w1', 'L0_ffn_b1', 'L0_ffn_alpha_w1', 'L0_ffn_alpha_a1',
        'L0_ffn_w2', 'L0_ffn_b2', 'L0_ffn_alpha_w2', 'L0_ffn_alpha_a2']


def positions():
    import numpy as np
    at = np.arange(SEQ, dtype=np.float32)[:, None]
    ids = np.arange(C, dtype=np.float32)[None, :]
    even_exp = np.floor(ids / np.float32(2.0)) * np.float32(2.0) / np.float32(C)
    angle = at / np.power(np.float32(10000.0), even_exp)
    return np.where(np.arange(C) % 2 == 0, np.sin(angle), np.cos(angle)).astype(np.float32)


def kernel(**inputs):
    import numpy as np
    import concourse.bacc as bacc
    from concourse.bass_utils import run_bass_kernel_spmd

    nc = bacc.Bacc("TRN2", target_bir_lowering=False, num_devices=1)
    arrays, args = {}, []
    for name, a in [(n, inputs[n]) for n in _INS] + [("positions", positions())]:
        a = np.ascontiguousarray(a)
        arrays[f"in_{name}"] = a
        args.append(nc.dram_tensor(f"in_{name}", a.shape, mybir.dt.from_np(a.dtype), kind="ExternalInput").ap())
    out = nc.dram_tensor("out", (B, SEQ, C), F32, kind="ExternalOutput").ap()
    layer(nc, *args, out)
    r = run_bass_kernel_spmd(nc, [arrays], core_ids=[0])
    return r.results[0]["out"]
```

```python
from contextlib import ExitStack

import concourse.bass as bass
from concourse import mybir

F32 = mybir.dt.float32
F16 = mybir.dt.float16
BF16 = mybir.dt.bfloat16
I32 = mybir.dt.int32
ALU = mybir.AluOpType
ACT = mybir.ActivationFunctionType
X = mybir.AxisListType.X

P = 128
B, SEQ = 8, 1024
C = 192
H, D = 12, 16
HID = 768
TB = SEQ // P
TH = TB // 2
NQ = TH * P
HALVES = 2 * B
KC = C // 2
HB = HID // P
WB = 3 * C // KC
GH = 4
HG = H // GH
VE = D + 1
VW = H * VE + 2 * D - VE
GROUPS = 2 * H
UNITS = HG * TB
EPS = 1e-5
QN, QP = -8.0, 7.0
GELU_CLIP = 10.0
ROUND = 1.5 * 2.0 ** 23
MAGIC = float(0x5F3759DF)
QK_SCALE = 64.0
SCORE_SCALE = D ** -0.5 / QK_SCALE ** 2

PLAN = """
Y0 ; Y1
Y2 ; Y3
F0 ; F1
F2 ; F3 G0
G1 P0 ; G2
G3 H0 ; H1
H2 ; H3 l0
;
; R0 m0 N0
;
;
; I0 I1
I2 I3 A0 ; A1 A2
X0 X1 B0 ; A3 B1 X2 X3 r0 B2 X4 X5 r1 B3 C0 C1 C2 r2 r3 S0 n0
;
C3 n1 x0 ;
; x1
; D0
E0 n2 ; D1
x2 E1 n3 ;
; D2
E2 x3 ; D3
E3 x4 x5 ;
"""
JOB_KINDS = "ABCDEFGHIXY"
UNIT_WORK = [[[(w[0], int(w[1])) for w in half.split()] for half in line.split(";")]
             for line in PLAN.strip().split("\n")]
UNIT_WORK += [[[], []]] * (UNITS - len(UNIT_WORK))
WORK = [w for unit in UNIT_WORK for part in unit for w in part]
JOBS = [w for w in WORK if w[0] in JOB_KINDS]
X_UNIT = next(u for u, unit in enumerate(UNIT_WORK) if ("X", 0) in unit[0])
BANKS = 3
ACT_SQUARES = (-2, -1, 0)
IN_TURN = [w for w in JOBS if w[0] not in "XB"]
LAG = {**dict.fromkeys("PNABCDE", 2), **dict.fromkeys("FGHIX", -1), "Y": -2}
PER_HALF = {**dict.fromkeys("ABCDEFGHIY", TH), "X": HB}
EVACS = {"E": 2}


def job_half(kind, s):
    return s + LAG[kind]


def job_runs(kind, s0):
    return 0 <= job_half(kind, s0) < HALVES


def bank_of(job):
    kind, t = job
    return {"X": t % 2, "B": 2}[kind] if kind in "XB" else IN_TURN.index(job) % BANKS


def job_before(job, s0):
    at = JOBS.index(job)
    for back in (0, 1):
        for other in reversed(JOBS[:at] if back == 0 else JOBS):
            if bank_of(other) == bank_of(job) and job_runs(other[0], s0 - back):
                return other, back
    return None


def layer(nc, x_tok, x_seg, tok_table, seg_table, w_qkv, w_proj, w1, b1, aw1, aa1, w2, b2, aw2, aa2,
          pos, out):
    ctx = ExitStack()
    with ctx:
        def sb(name, shape, dt=F32):
            return ctx.enter_context(nc.sbuf_tensor(name, shape, dt))

        def sem(name):
            return ctx.enter_context(nc.semaphore(name))

        h_all = sb("h_all", [P, B * TB * C])
        probs = sb("probs", [P, 2, GH, NQ])
        qT = sb("qT", [P, 2, H // 2, SEQ], F16)
        kA = sb("kA", [P, 2, H // 2, SEQ], F16)
        kB = sb("kB", [P, 2, H // 2, SEQ], F16)
        v_sb = sb("v_sb", [P, 2, TB, VW])
        o_nat = sb("o_nat", [P, TH, C])
        hT = sb("hT", [KC, TH, 2, P])
        stack = sb("stack", [P, 2, 2, H, 4, D], F16)
        o_sb = sb("o_sb", [P, HG, NQ])
        gelu = sb("gelu", [P, HB, NQ])
        hq = sb("hq", [P, HB, NQ], BF16)
        sq = sb("sq", [P, 2, 2 * C])
        hn, oT = o_nat, hT
        qk = [o_nat[:, 2 * t:2 * t + 2].rearrange("p t c -> p (t c)") for t in range(2)]
        hq_tail = hq[:, HB // 2:HB].rearrange("p j n -> p (j n)").bitcast(F32)
        qk += [hq_tail[:, t * 2 * C:(t + 1) * 2 * C] for t in range(2)]
        qkn = sq[:, 0]
        xq = sq[:, 1].bitcast(BF16).rearrange("p (t c) -> p t c", c=C)
        stack_f = stack[:].rearrange("p s n h a d -> p (s n h a d)")
        xqT = stack_f[0:KC, 0:2 * NQ].bitcast(BF16).rearrange("p (k n) -> p k n", k=2)
        gelu_f = gelu[:].rearrange("p j n -> p (j n)")
        xf = gelu_f[:, 0:TH * C].rearrange("p (t c) -> p t c", c=C)
        y_sb = gelu_f[:, TH * C:2 * TH * C].rearrange("p (t c) -> p t c", c=C)
        st, mv = sb("st", [P, 2, TH, 6]), sb("mv", [P, 2, TH, 2])
        vn, rn, wn = (sb(n, [P, 2, TH]) for n in ("vn", "rn", "wn"))
        vq, rq, wq_ = (sb(n, [P, TH, GROUPS]) for n in ("vq", "rq", "wq_"))
        ra2 = sb("ra2", [P, TH])
        rsum = sb("rsum", [P, H])
        gate_sb = sb("gate_sb", [P, 1])
        wT = sb("wT", [KC, 2, 3 * C])
        wmean = sb("wmean", [KC, 2, GROUPS])
        wpT = sb("wpT", [KC, 2, C])
        w1T = sb("w1T", [KC, 2, HID], BF16)
        w2T = sb("w2T", [P, HB, C], BF16)
        a1, ia1, a2, ia2 = (sb(n, [P, 1]) for n in ("a1", "ia1", "a2", "ia2"))
        bound, qlo, qhi = (sb(n, [P, 1]) for n in ("bound", "qlo", "qhi"))
        aw1_sb, iaw1, s1_sb, b1_sb = (sb(n, [P, HB]) for n in ("aw1_sb", "iaw1", "s1_sb", "b1_sb"))
        aw2c, iaw2 = sb("aw2c", [KC, 2]), sb("iaw2", [KC, 2])
        s2_row, b2_row = sb("s2_row", [P, C]), sb("b2_row", [P, C])
        ident = sb("ident", [P, P])
        ident_h = sb("ident_h", [P, P], F16)
        ident_b = sb("ident_b", [P, P], BF16)
        idx_in = sb("idx_in", [P, 2, B, TB], I32)
        idx_f = sb("idx_f", [P, 2, B, TB])
        idx = sb("idx", [P, 2, B * TB], I32)
        start_f = probs[:].rearrange("p a g n -> p (a g n)")
        hq_f = hq[:].rearrange("p j n -> p (j n)")
        wq_nat = start_f[0:KC, 0:WB * C].rearrange("p (r c) -> p r c", c=C)
        wp_nat = start_f[0:KC, WB * C:(WB + 2) * C].rearrange("p (r c) -> p r c", c=C)
        aa1_in = start_f[:, (WB + 2) * C:(WB + 3) * C]
        aa2_in = start_f[:, (WB + 3) * C:(WB + 3) * C + HID]
        w1_nat = gelu_f[:, 0:HB * C].rearrange("p (j c) -> p j c", c=C)
        w2_nat = gelu_f[0:KC, HB * C:HB * C + 2 * HID].rearrange("p (r h) -> p r h", h=HID)
        w1_q = hq_f[:, 0:HB * C].rearrange("p (j c) -> p j c", c=C)
        w2_q = hq_f[0:KC, HB * C:HB * C + 2 * HID].rearrange("p (r h) -> p r h", h=HID)

        ps_s = ctx.enter_context(nc.psum_tensor("ps_s", [P, GH, NQ], F32))
        ps_o = ctx.enter_context(nc.psum_tensor("ps_o", [P, NQ], F32))
        ps_j = ctx.enter_context(nc.psum_tensor("ps_j", [P, BANKS, 512], F32))

        idx_loaded, w_loaded, aw_loaded = sem("idx_loaded"), sem("w_loaded"), sem("aw_loaded")
        pos_loaded = sem("pos_loaded")
        seg_added, tok_added = ([sem(f"{n}{i}") for i in range(2)] for n in ("seg_added", "tok_added"))
        idx_ready, ident_ready, filled = sem("idx_ready"), sem("ident_ready"), sem("filled")
        pool_step, dve_step = sem("pool_step"), sem("dve_step")
        weights_q, weights_mm, weights_ready = sem("weights_q"), sem("weights_mm"), sem("weights_ready")
        hn_ready, stack_ready, xq_ready, hq_ready = (
            sem(n) for n in ("hn_ready", "stack_ready", "xq_ready", "hq_ready"))
        scores_mm, exp_done, heads_mm, heads_out = (
            sem(n) for n in ("scores_mm", "exp_done", "heads_mm", "heads_out"))
        squared, summed = sem("squared"), sem("summed")
        out_ready, stored = sem("out_ready"), sem("stored")
        job_mm = {k: sem(f"{k}_mm") for k in PER_HALF}
        job_out = {k: sem(f"{k}_out") for k in PER_HALF}

        def nth(half, t, per):
            return half * per + (t + 1)

        def out_count(job, half):
            kind, t = job
            return (half * PER_HALF[kind] + (t + 1)) * EVACS.get(kind, 1)

        def h_tile(half, t):
            return h_all[:, bass.ds(half * (TH * C) + t * C, C)]

        def bank(job):
            return ps_j[:, bank_of(job), :]

        def bank16(job, dt):
            return ps_j[:, bank_of(job), :].bitcast(dt)

        def attends(s0):
            return 0 <= s0 < HALVES

        def halfsteps(eng, one):
            for s in range(-2, 2):
                one(s, s, s // 2)
            with eng.Fori(0, (B - 2) // 2) as turn:
                for k in range(4):
                    one(2 + k, turn * 4 + (2 + k), turn * 2 + (1 + k // 2))
            for s in range(HALVES - 2, HALVES + 2):
                one(s, s, s // 2)

        block = ctx.enter_context(nc.Block())

        @block.sync
        def _(sp):
            sp.dma_start(idx_in[:, 0], x_tok.rearrange("b (p j) -> p b j", j=TB)).then_inc(idx_loaded, 16)
            sp.dma_start(idx_in[:, 1], x_seg.rearrange("b (p j) -> p b j", j=TB)).then_inc(idx_loaded, 16)
            pos_v = pos.rearrange("(p j) c -> p (j c)", j=TB)

            def load_pos(b):
                sp.dma_start(h_all[:, b * TB * C:(b + 1) * TB * C], pos_v).then_inc(pos_loaded, 16)
                sp.wait_ge(pos_loaded, 16 * (b + 1))

            load_pos(0)
            sp.dma_start(wq_nat, w_qkv.rearrange("(r p) c -> p r c", p=KC)).then_inc(w_loaded, 16)
            sp.dma_start(wp_nat, w_proj.rearrange("(r p) c -> p r c", p=KC)).then_inc(w_loaded, 16)
            sp.dma_start(w1_nat, w1.rearrange("(p j) c -> p j c", j=HB)).then_inc(w_loaded, 16)
            sp.dma_start(w2_nat, w2.rearrange("(p r) h -> p r h", r=2)).then_inc(w_loaded, 16)
            for b in range(1, B):
                load_pos(b)

            def one(s0, s, b):
                if not job_runs("Y", s0):
                    return
                y = job_half("Y", s)
                sp.wait_ge(out_ready, nth(y, 0, 1))
                sp.dma_start(out_rows[:, bass.ds(b - 1, 1), s0 % 2 * TH * C:(s0 % 2 + 1) * TH * C],
                             h_all[:, bass.ds(y * (TH * C), TH * C)]).then_inc(stored, 16)

            out_rows = out.rearrange("b (p j) c -> p b (j c)", j=TB)
            halfsteps(sp, one)
            sp.wait_ge(stored, 16 * HALVES)

        @block.gpsimd
        def _(pool):
            def gather(table, which, half, done):
                for j in range(TH):
                    t = half * TH + j
                    nc.gpsimd.indirect_dma_start(
                        out=h_all[:, t * C:(t + 1) * C], out_offset=None, in_=table,
                        in_offset=bass.IndirectOffsetOnAxis(ap=idx[:, which, t:t + 1], axis=0),
                        compute_op=ALU.add).then_inc(done, 16)

            for m in (ident, ident_h, ident_b):
                nc.gpsimd.memset(m[:], 0.0).then_inc(pool_step, 1)
            for n, m in enumerate((ident, ident_h, ident_b)):
                pool.wait_ge(pool_step, n + 1)
                nc.gpsimd.affine_select(out=m[:], in_=m[:], compare_op=ALU.not_equal, fill=1.0, base=0,
                                        pattern=[[-1, P]], channel_multiplier=1).then_inc(ident_ready, 1)

            def fill(n, dst, value):
                if n == 0:
                    pool.wait_ge(ident_ready, 3)
                else:
                    pool.wait_ge(filled, n)
                nc.gpsimd.memset(dst, value).then_inc(filled, 1)

            def constant_parts(b):
                fill(3 * b, kA[P // 2:P, b].bitcast(F32), 0.0)
                fill(3 * b + 1, kB[0:P // 2, b].bitcast(F32), 0.0)
                fill(3 * b + 2, v_sb[:, b], 1.0)

            pool.wait_ge(idx_ready, 1)
            for half in range(HALVES + 1):
                if half < HALVES:
                    pool.wait_ge(pos_loaded, 16 * (half // 2 + 1))
                    gather(seg_table, 1, half, seg_added[half % 2])
                    if half < 2:
                        constant_parts(half)
                if half:
                    prior = half - 1
                    pool.wait_ge(seg_added[prior % 2], 16 * TH * (prior // 2 + 1))
                    if prior >= 2:
                        pool.wait_ge(tok_added[prior % 2], 16 * TH * (prior // 2))
                    gather(tok_table, 0, prior, tok_added[prior % 2])

            def square(s0, s):
                if not job_runs("B", s0) or s0 in ACT_SQUARES:
                    return
                half = job_half("B", s)
                for t in range(TH):
                    pool.wait_ge(job_out["B"], nth(half, t, TH))
                    if job_half("B", s0) or t >= 2:
                        pool.wait_ge(summed, half * TH + (t - 1))
                    nc.gpsimd.tensor_tensor(sq[:, t % 2], qk[t], qk[t], ALU.mult).then_inc(squared, 1)

            def add_result(s0, s):
                if not job_runs("Y", s0):
                    return
                y = job_half("Y", s)
                pool.wait_ge(job_out["Y"], nth(y, TH - 1, TH))
                nc.gpsimd.tensor_tensor(y_sb, y_sb, b2_row[:].unsqueeze(1).broadcast_to([P, TH, C]),
                                        ALU.add).then_inc(pool_step, 1)
                pool.wait_ge(pool_step, y + 4)
                hv = h_all[:, bass.ds(y * (TH * C), TH * C)]
                nc.gpsimd.tensor_tensor(hv, hv, gelu_f[:, TH * C:2 * TH * C],
                                        ALU.add).then_inc(out_ready, 1)

            def one(s0, s, b):
                add_result(s0, s)
                square(s0, s)

            halfsteps(pool, one)

        @block.scalar
        def _(act):
            act.dma_start(aa1_in, aa1.unsqueeze(0).broadcast_to([P, C])).then_inc(aw_loaded, 16)
            act.dma_start(aa2_in, aa2.unsqueeze(0).broadcast_to([P, HID])).then_inc(aw_loaded, 16)
            act.dma_start(aw1_sb[:], aw1.rearrange("(p j) -> p j", j=HB)).then_inc(aw_loaded, 16)
            act.dma_start(b1_sb[:], b1.rearrange("(p j) -> p j", j=HB)).then_inc(aw_loaded, 16)
            act.dma_start(aw2c[:], aw2.rearrange("(p r) -> p r", r=2)).then_inc(aw_loaded, 16)
            act.dma_start(s2_row[:], aw2.unsqueeze(0).broadcast_to([P, C])).then_inc(aw_loaded, 16)
            act.dma_start(b2_row[:], b2.unsqueeze(0).broadcast_to([P, C])).then_inc(aw_loaded, 16)
            act.wait_ge(weights_ready, 1)

            def square(s0, s, t):
                half = job_half("B", s)
                act.wait_ge(job_out["B"], nth(half, t, TH))
                if job_half("B", s0) or t >= 2:
                    act.wait_ge(summed, half * TH + (t - 1))
                nc.scalar.activation(sq[:, t % 2], qk[t], ACT.Square).then_inc(squared, 1)

            def q_out(s0, s, t):
                p0 = job_half("D", s0)
                tile = p0 % 2 * TH + t
                act.wait_ge(job_mm["D"], nth(job_half("D", s), t, TH))
                nc.scalar.activation(qT[:, p0 // 2 % 2, :, tile * P:(tile + 1) * P],
                                     bank16(("D", t), F16)[:, 0:H // 2 * P].rearrange("p (i n) -> p i n", n=P),
                                     ACT.Copy).then_inc(job_out["D"], 1)

            def gelu_out(s0, s, j):
                half = job_half("X", s)
                act.wait_ge(job_mm["X"], nth(half, j, HB))
                if j == 0 and job_runs("Y", s0):
                    act.wait_ge(out_ready, nth(job_half("Y", s), 0, 1))
                nc.scalar.activation(gelu[:, j], bank(("X", j)), ACT.Gelu, bias=b1_sb[:, j:j + 1],
                                     scale=s1_sb[:, j:j + 1]).then_inc(job_out["X"], 1)

            def exps(s0, s, u, pair):
                act.wait_ge(scores_mm, 2 * UNITS * s + (2 * u + pair + 1))
                nc.scalar.activation(probs[:, u % 2, 2 * pair:2 * pair + 2], ps_s[:, 2 * pair:2 * pair + 2],
                                     ACT.Exp, scale=SCORE_SCALE).then_inc(exp_done, 1)

            def one(s0, s, b):
                for u in range(UNITS):
                    work = UNIT_WORK[u]
                    if u == X_UNIT and job_runs("X", s0):
                        for j in range(HB):
                            gelu_out(s0, s, j)
                    for pair in range(2):
                        if attends(s0):
                            exps(s0, s, u, pair)
                        for kind, t in work[pair]:
                            if kind == "B" and s0 in ACT_SQUARES:
                                square(s0, s, t)
                            if kind == "D" and job_runs("D", s0):
                                q_out(s0, s, t)

            halfsteps(act, one)

        @block.vector
        def _(dve):
            steps = {"done": 0, "turns": 0}

            def link(ins):
                steps["done"] += 1
                ins.then_inc(dve_step, 1)
                dve.wait_ge(dve_step, steps["turns"] + steps["done"])

            ts = nc.vector.tensor_scalar
            tt = nc.vector.tensor_tensor
            stt = nc.vector.scalar_tensor_tensor

            def rsqrt(y, v, w):
                link(ts(w.bitcast(I32), v.bitcast(I32), 1, None, ALU.logical_shift_right))
                link(ts(y.bitcast(I32), w.bitcast(I32), -1.0, MAGIC, ALU.mult, ALU.add))
                for _ in range(3):
                    link(stt(out=w, in0=y, scalar=-0.5, in1=y, op0=ALU.mult, op1=ALU.mult))
                    link(tt(w, w, v, ALU.mult))
                    link(stt(out=y, in0=w, scalar=1.5, in1=y, op0=ALU.add, op1=ALU.mult))

            def gate():
                nc.vector.memset(gate_sb[:], 0.0)

            def norm_stats(which, half):
                gate()
                for t in range(TH):
                    last = nc.vector.bn_stats(st[:, which, t], h_tile(half, t))
                link(last)
                gate()
                for t in range(TH):
                    last = nc.vector.bn_aggr(mv[:, which, t], st[:, which, t])
                link(last)
                link(ts(vn[:, which], mv[:, which, :, 1], EPS, None, ALU.add))

            def norm_roots(s0):
                lo = 0 if job_runs("P", s0) else 1
                hi = 2 if job_runs("H", s0) else 1
                if lo < hi:
                    rsqrt(rn[:, lo:hi], vn[:, lo:hi], wn[:, lo:hi])

            def first_norm(s0, s):
                half = job_half("N", s)
                for t in range(TH):
                    ts(hn[:, t], h_tile(half, t), mv[:, 0, t, 0:1], rn[:, 0, t:t + 1],
                       ALU.subtract, ALU.mult).then_inc(hn_ready, 1)

            def quantise(dst, src, tmp, lo, hi):
                link(ts(tmp, src, lo, hi, ALU.max, ALU.min))
                return ts(dst, tmp, ROUND, -ROUND, ALU.add, ALU.add)

            def copy_out(job, half, dst, src):
                dve.wait_ge(job_mm[job[0]], nth(half, job[1], PER_HALF[job[0]]))
                nc.vector.tensor_copy(dst, src).then_inc(job_out[job[0]], 1)

            def squares_sum(s0, s, t):
                half = job_half("B", s)
                dve.wait_ge(squared, nth(half, t, TH))
                nc.vector.tensor_reduce(vq[:, t], sq[:, t % 2].rearrange("p (g d) -> p g d", d=D),
                                        X, ALU.add).then_inc(summed, 1)

            def qk_roots(s0, s):
                dve.wait_ge(summed, nth(job_half("B", s), TH - 1, TH))
                link(ts(vq[:], vq[:], 1.0 / (D * QK_SCALE ** 2), EPS / QK_SCALE ** 2, ALU.mult, ALU.add))
                rsqrt(rq[:], vq[:], wq_[:])

            def split_qk(s0, s, t):
                half, h0 = job_half("D", s), job_half("D", s0)
                g = lambda a: a.rearrange("p (g d) -> p g d", d=D)
                if TH * h0 + t:
                    dve.wait_ge(stack_ready, half * TH + t)
                link(tt(g(qkn), g(qk[t]), rq[:, t, 0:GROUPS].unsqueeze(2).broadcast_to([P, GROUPS, D]), ALU.mult))
                if t == 0 and job_runs("X", s0):
                    dve.wait_ge(job_mm["X"], nth(job_half("X", s), HB - 1, HB))
                if TH * h0 + t >= 2:
                    dve.wait_ge(job_mm["E"], half * TH + (t - 1))
                for n, (hi, lo) in enumerate((((0, 2, 1), (2, 4, 1)), ((0, 4, 2), (1, 4, 2)))):
                    src = qkn[:, n * C:(n + 1) * C].rearrange("p (h d) -> p h d", d=D)
                    src = src.unsqueeze(2).broadcast_to([P, H, 2, D])
                    part = stack[:, t % 2, n]
                    high = part[:, :, hi[0]:hi[1]:hi[2], :]
                    nc.vector.tensor_copy(high, src).then_inc(dve_step, 1)
                    steps["done"] += 1
                dve.wait_ge(dve_step, steps["turns"] + steps["done"])
                for n, (hi, lo) in enumerate((((0, 2, 1), (2, 4, 1)), ((0, 4, 2), (1, 4, 2)))):
                    src = qkn[:, n * C:(n + 1) * C].rearrange("p (h d) -> p h d", d=D)
                    src = src.unsqueeze(2).broadcast_to([P, H, 2, D])
                    part = stack[:, t % 2, n]
                    high = part[:, :, hi[0]:hi[1]:hi[2], :]
                    last = tt(part[:, :, lo[0]:lo[1]:lo[2], :], src, high, ALU.subtract)
                last.then_inc(stack_ready, 1)

            def head_outputs(s0, s, group):
                dve.wait_ge(heads_mm, UNITS * s + TB * (group + 1))
                nc.vector.tensor_copy(o_sb[:, group], ps_o[:]).then_inc(heads_out, 1)

            def second_norm(s0, s):
                half = job_half("I", s)
                link(ts(ra2[:], rn[:, 1], ia1[:], None, ALU.mult))
                for t in range(TH):
                    last = ts(xf[:, t], h_tile(half, t), mv[:, 1, t, 0:1], ra2[:, t:t + 1],
                              ALU.subtract, ALU.mult)
                link(last)
                quantise(xq, xf, xf, QN, QP).then_inc(xq_ready, 1)

            def quantise_gelu(s0, s, t):
                dve.wait_ge(job_out["X"], nth(job_half("X", s), t, HB))
                link(ts(gelu[:, t], gelu[:, t], ia2[:], qlo[:], ALU.mult, ALU.max))
                link(ts(gelu[:, t], gelu[:, t], qhi[:], ROUND, ALU.min, ALU.add))
                ts(hq[:, t], gelu[:, t], ROUND, None, ALU.subtract).then_inc(hq_ready, 1)

            def job_result(s0, s, kind, t):
                if not job_runs(kind, s0):
                    return
                half, h0 = job_half(kind, s), job_half(kind, s0)
                job = (kind, t)
                ps = bank(job)
                tile = h0 % 2 * TH + t
                par = h0 // 2 % 2
                if kind == "A":
                    copy_out(job, half, hT[:, t], ps[0:KC, 0:2 * P].rearrange("p (k n) -> p k n", k=2))
                if kind == "B":
                    copy_out(job, half, qk[t], ps[:, 0:2 * C])
                if kind == "C":
                    if t == 0 and h0 in (0, 2):
                        dve.wait_ge(filled, 3 * (h0 // 2 + 1))
                    copy_out(job, half, v_sb[:, par, tile, 0:H * VE].rearrange("p (h e) -> p h e", e=VE)[:, :, 0:D],
                             ps[:, 0:C].rearrange("p (h d) -> p h d", d=D))
                if kind == "E":
                    for lo, dst in ((0, kA), (P // 2, kB)):
                        copy_out(job, half, dst[lo:lo + P // 2, par, :, tile * P:(tile + 1) * P],
                                 bank16(job, F16)[lo:lo + P // 2, 0:HB * P].rearrange("p (i n) -> p i n", n=P))
                if kind == "F":
                    dve.wait_ge(job_mm["F"], nth(half, t, TH))
                    heads = ps[:, 0:H * 2 * D].rearrange("p (h e) -> p h e", e=2 * D)
                    if h0 or t:
                        dve.wait_ge(job_out["F"], half * TH + t)
                    link(nc.vector.reciprocal(rsum[:], heads[:, :, D]))
                    tt(o_nat[:, t].rearrange("p (h d) -> p h d", d=D), heads[:, :, 0:D],
                       rsum[:].unsqueeze(2).broadcast_to([P, H, D]), ALU.mult).then_inc(job_out["F"], 1)
                if kind == "G":
                    copy_out(job, half, oT[:, t], ps[0:KC, 0:2 * P].rearrange("p (k n) -> p k n", k=2))
                if kind == "H":
                    dve.wait_ge(job_mm["H"], nth(half, t, TH))
                    tt(h_tile(half, t), ps[:, 0:C], h_tile(half, t), ALU.add).then_inc(job_out["H"], 1)
                    if t == TH - 1:
                        dve.wait_ge(job_out["H"], nth(half, t, TH))
                if kind == "I":
                    copy_out(job, half, xqT[:, :, t * P:(t + 1) * P],
                             bank16(job, BF16)[0:KC, 0:2 * P].rearrange("p (k n) -> p k n", k=2))
                if kind == "Y":
                    dve.wait_ge(job_mm["Y"], nth(half, t, TH))
                    if h0 >= 1 and t == 0:
                        dve.wait_ge(out_ready, nth(half - 1, 0, 1))
                    tt(y_sb[:, t], ps[:, 0:C], s2_row[:], ALU.mult).then_inc(job_out["Y"], 1)

            def start():
                dve.wait_ge(idx_loaded, 32)
                for w, rows in ((0, tok_table.shape[0]), (1, seg_table.shape[0])):
                    link(ts(idx_f[:, w], idx_in[:, w], 0.0, float(rows), ALU.is_lt, ALU.mult))
                    link(tt(idx_f[:, w], idx_f[:, w], idx_in[:, w], ALU.add))
                    last = ts(idx[:, w], idx_f[:, w].rearrange("p b j -> p (b j)"), 0.0, float(rows - 1),
                              ALU.max, ALU.min)
                last.then_inc(idx_ready, 1)
                dve.wait_ge(aw_loaded, 16 * 7)
                for a, ia, src, n in ((a1, ia1, aa1_in, C), (a2, ia2, aa2_in, HID)):
                    link(nc.vector.tensor_reduce(a[:], src, X, ALU.add))
                    link(ts(a[:], a[:], 1.0 / n, None, ALU.mult))
                    link(nc.vector.reciprocal(ia[:], a[:]))
                link(ts(bound[:], ia2[:], -GELU_CLIP, None, ALU.mult))
                link(stt(out=bound[:], in0=ia2[:], scalar=GELU_CLIP, in1=bound[:], op0=ALU.mult, op1=ALU.max))
                link(ts(qhi[:], bound[:], QP, None, ALU.min))
                link(ts(qlo[:], bound[:], -1.0, QN, ALU.mult, ALU.max))
                link(ts(s1_sb[:], aw1_sb[:], a1[:], None, ALU.mult))
                link(ts(s2_row[:], s2_row[:], a2[:], None, ALU.mult))
                link(nc.vector.reciprocal(iaw1[:], aw1_sb[:]))
                link(nc.vector.reciprocal(iaw2[:], aw2c[:]))
                dve.wait_ge(w_loaded, 16 * 4)
                for nat, q, ia, n in ((w1_nat, w1_q, iaw1, HB), (w2_nat, w2_q, iaw2, 2)):
                    for j in range(n):
                        last = ts(nat[:, j], nat[:, j], ia[:, j:j + 1], None, ALU.mult)
                    link(last)
                    quantise(q, nat, nat, QN, QP).then_inc(weights_q, 1)
                dve.wait_ge(weights_mm, 1)
                for k in range(2):
                    last = nc.vector.tensor_copy(wT[:, k, 0:2 * C], ps_j[0:KC, k, 0:2 * C])
                last = nc.vector.tensor_copy(wT[:, :, 2 * C:3 * C],
                                             ps_j[0:KC, 2, 0:2 * C].rearrange("p (k c) -> p k c", k=2))
                link(last)
                nc.vector.tensor_copy(wpT[:], ps_o[0:KC, 0:2 * C].rearrange("p (k c) -> p k c", k=2))
                for k in range(2):
                    g = wT[:, k, 0:2 * C].rearrange("p (g d) -> p g d", d=D)
                    link(nc.vector.tensor_reduce(wmean[:, k], g, X, ALU.add))
                    link(ts(wmean[:, k], wmean[:, k], -1.0 / D, None, ALU.mult))
                    link(tt(g, g, wmean[:, k].unsqueeze(2).broadcast_to([KC, GROUPS, D]), ALU.add))
                dve.wait_ge(weights_mm, 2)
                for k in range(2):
                    nc.vector.tensor_copy(w1T[:, k], ps_s[0:KC, k].bitcast(BF16)[:, 0:HID])
                for lo, n in ((0, 4), (4, 2)):
                    for j in range(n):
                        last = nc.vector.tensor_copy(
                            w2T[:, lo + j].rearrange("p (c r) -> p c r", r=2),
                            ps_s[:, 2 + lo // 4].bitcast(BF16)[:, j * C:(j + 1) * C].rearrange("p (r c) -> p c r", r=2))
                link(last)
                nc.vector.tensor_copy(a1[:], a1[:]).then_inc(weights_ready, 1)

            def one(s0, s):
                for u in range(UNITS):
                    for n, work in enumerate(UNIT_WORK[u]):
                        if n == 1 and u % TB == 0:
                            if u == 0 and attends(s0 - 1):
                                head_outputs(s0 - 1, s - 1, HG - 1)
                            elif u and attends(s0):
                                head_outputs(s0, s, u // TB - 1)
                        for kind, t in work:
                            if kind == "P" and job_runs("P", s0):
                                p = job_half("P", s)
                                dve.wait_ge(tok_added[s0 % 2], (p - s0 % 2 + 2) * (TH * 8))
                                norm_stats(0, p)
                            elif kind == "l" and job_runs("H", s0):
                                norm_stats(1, job_half("H", s))
                            elif kind == "R":
                                norm_roots(s0)
                            elif kind == "N" and job_runs("N", s0):
                                first_norm(s0, s)
                            elif kind == "m" and job_runs("I", s0):
                                second_norm(s0, s)
                            elif kind == "r" and job_runs("B", s0):
                                squares_sum(s0, s, t)
                            elif kind == "S" and job_runs("B", s0):
                                qk_roots(s0, s)
                            elif kind == "n" and job_runs("D", s0):
                                split_qk(s0, s, t)
                            elif kind == "x" and job_runs("X", s0):
                                quantise_gelu(s0, s, t)
                            elif kind in job_out:
                                job_result(s0, s, kind, t)

            start()
            for s in range(-2, 2):
                one(s, s)
            before = steps["done"]
            with dve.Fori(0, (B - 2) // 2) as turn:
                steps["turns"] = turn * LINKS_PER_TURN
                for k in range(4):
                    one(2 + k, turn * 4 + (2 + k))
            assert steps["done"] - before == LINKS_PER_TURN, steps["done"] - before
            steps["turns"] = ((B - 2) // 2 - 1) * LINKS_PER_TURN
            for s in range(HALVES - 2, HALVES + 2):
                one(s, s)

        @block.tensor
        def _(pe):
            mm = nc.tensor.matmul

            def start():
                pe.wait_ge(ident_ready, 3)
                pe.wait_ge(w_loaded, 16 * 4)
                for k in range(2):
                    cols = slice(k * KC, (k + 1) * KC)
                    for r in range(4):
                        nc.tensor.transpose(ps_j[0:KC, k, r * KC:(r + 1) * KC], wq_nat[:, r, cols], ident[0:KC, 0:KC])
                    for r in range(2):
                        nc.tensor.transpose(ps_j[0:KC, 2, k * C + r * KC:k * C + (r + 1) * KC],
                                            wq_nat[:, 4 + r, cols], ident[0:KC, 0:KC])
                    for r in range(2):
                        last = nc.tensor.transpose(ps_o[0:KC, k * C + r * KC:k * C + (r + 1) * KC],
                                                   wp_nat[:, r, cols], ident[0:KC, 0:KC])
                last.then_inc(weights_mm, 1)
                pe.wait_ge(weights_q, 2)
                for k in range(2):
                    for j in range(HB):
                        nc.tensor.transpose(ps_s[0:KC, k].bitcast(BF16)[:, j * P:(j + 1) * P],
                                            w1_q[:, j, k * KC:(k + 1) * KC], ident_b[:])
                for j in range(HB):
                    for r in range(2):
                        at = j % 4 * C + r * KC
                        last = nc.tensor.transpose(ps_s[:, 2 + j // 4].bitcast(BF16)[:, at:at + KC],
                                                   w2_q[:, r, j::HB], ident_b[0:KC, 0:KC])
                last.then_inc(weights_mm, 1)
                pe.wait_ge(weights_ready, 1)

            def scores(s0, s, u):
                par, nh = s0 // 2 % 2, s0 % 2
                group, m = divmod(u, TB)
                if u == 0 and nh == 0:
                    if s0 <= 2:
                        pe.wait_ge(filled, 3 * (s0 // 2 + 1))
                    pe.wait_ge(job_out["D"], (s + 2) * TH)
                    pe.wait_ge(job_out["E"], (s + 2) * TH * 2)
                for j in range(GH):
                    if j % 2 == 0 and (u or attends(s0 - 1)):
                        pe.wait_ge(exp_done, 2 * UNITS * s + (2 * u - 1 + j // 2))
                    head = GH * group + j
                    k = kA if head % 2 == 0 else kB
                    last = mm(ps_s[:, j], k[:, par, head // 2, m * P:(m + 1) * P],
                              qT[:, par, head // 2, nh * NQ:(nh + 1) * NQ], start=True, stop=True)
                    if j % 2:
                        last.then_inc(scores_mm, 1)

            def heads(s0, s, u):
                par = s0 // 2 % 2
                group, m = divmod(u, TB)
                if u == 0 and s0 % 2 == 0:
                    pe.wait_ge(job_out["C"], (s + 2) * TH)
                if m == 0 and (group or attends(s0 - 1)):
                    pe.wait_ge(heads_out, HG * s + group)
                pe.wait_ge(exp_done, 2 * UNITS * s + (2 * u + 2))
                for j in range(GH):
                    last = mm(ps_o[32 * j:32 * j + 2 * D, :], v_sb[:, par, m, (GH * group + j) * VE:(GH * group + j) * VE + 2 * D],
                              probs[:, u % 2, j], start=(m == 0), stop=(m == TB - 1))
                last.then_inc(heads_mm, 1)

            def job(s0, s, kind, t):
                if not job_runs(kind, s0):
                    return
                half, h0 = job_half(kind, s), job_half(kind, s0)
                prior = job_before((kind, t), s0)
                if prior:
                    (pk, pt), back = prior
                    pe.wait_ge(job_out[pk], out_count((pk, pt), job_half(pk, s - back)))
                ps = bank((kind, t))
                if kind == "A":
                    pe.wait_ge(hn_ready, nth(half, t, TH))
                    for k in range(2):
                        last = nc.tensor.transpose(ps[0:KC, k * P:(k + 1) * P], hn[:, t, k * KC:(k + 1) * KC], ident[:])
                if kind == "B":
                    pe.wait_ge(job_out["A"], nth(half, t, TH))
                if kind in "BC":
                    lo, hi = (0, 2 * C) if kind == "B" else (2 * C, 3 * C)
                    for k in range(2):
                        last = mm(ps[:, 0:hi - lo], hT[:, t, k], wT[:, k, lo:hi], start=(k == 0), stop=(k == 1))
                if kind in "DE":
                    pe.wait_ge(stack_ready, nth(half, t, TH))
                    for i in range(H // 2):
                        src = stack[:, t % 2, "DE".index(kind), 2 * i:2 * i + 2].rearrange("p h a d -> p (h a d)")
                        last = nc.tensor.transpose(bank16((kind, t), F16)[:, i * P:(i + 1) * P], src, ident_h[:])
                if kind == "F":
                    if t == 0:
                        pe.wait_ge(heads_out, nth(half, HG - 1, HG))
                    for g in range(HG):
                        last = nc.tensor.transpose(ps[:, g * P:(g + 1) * P], o_sb[:, g, t * P:(t + 1) * P], ident[:])
                if kind == "G":
                    pe.wait_ge(job_out["F"], nth(half, t, TH))
                    for k in range(2):
                        last = nc.tensor.transpose(ps[0:KC, k * P:(k + 1) * P], o_nat[:, t, k * KC:(k + 1) * KC], ident[:])
                if kind == "H":
                    pe.wait_ge(job_out["G"], nth(half, t, TH))
                    for k in range(2):
                        last = mm(ps[:, 0:C], oT[:, t, k], wpT[:, k], start=(k == 0), stop=(k == 1))
                if kind == "I":
                    if t == 0:
                        pe.wait_ge(xq_ready, nth(half, 0, 1))
                    for k in range(2):
                        last = nc.tensor.transpose(bank16((kind, t), BF16)[0:KC, k * P:(k + 1) * P],
                                                   xq[:, t, k * KC:(k + 1) * KC], ident_b[:])
                if kind == "X":
                    if t == 0:
                        pe.wait_ge(job_out["I"], nth(half, TH - 1, TH))
                    for k in range(2):
                        last = mm(ps, w1T[:, k, t * P:(t + 1) * P], xqT[:, k], start=(k == 0), stop=(k == 1))
                if kind == "Y":
                    if t == 0:
                        pe.wait_ge(hq_ready, nth(half, HB - 1, HB))
                    for j in range(HB):
                        last = mm(ps[:, 0:C], hq[:, j, t * P:(t + 1) * P], w2T[:, j], start=(j == 0), stop=(j == HB - 1))
                last.then_inc(job_mm[kind], 1)

            def one(s0, s, b):
                for u in range(UNITS):
                    first, second = UNIT_WORK[u]
                    if attends(s0):
                        scores(s0, s, u)
                    for kind, t in first:
                        if kind in job_mm:
                            job(s0, s, kind, t)
                    if u and attends(s0):
                        heads(s0, s, u - 1)
                    elif not u and attends(s0 - 1):
                        heads(s0 - 1, s - 1, UNITS - 1)
                    for kind, t in second:
                        if kind in job_mm:
                            job(s0, s, kind, t)

            start()
            halfsteps(pe, one)


LINKS_PER_TURN = 4 * 60


_INS = ['x', 'mask_BS_i2_0', 'L0_tok_token_table', 'L0_tok_segm_table', 'L0_attn_qkv_weight',
        'L0_attn_proj_weight', 'L0_ffn_w1', 'L0_ffn_b1', 'L0_ffn_alpha_w1', 'L0_ffn_alpha_a1',
        'L0_ffn_w2', 'L0_ffn_b2', 'L0_ffn_alpha_w2', 'L0_ffn_alpha_a2']


def positions():
    import numpy as np
    at = np.arange(SEQ, dtype=np.float32)[:, None]
    ids = np.arange(C, dtype=np.float32)[None, :]
    even_exp = np.floor(ids / np.float32(2.0)) * np.float32(2.0) / np.float32(C)
    angle = at / np.power(np.float32(10000.0), even_exp)
    return np.where(np.arange(C) % 2 == 0, np.sin(angle), np.cos(angle)).astype(np.float32)


def kernel(**inputs):
    import numpy as np
    import concourse.bacc as bacc
    from concourse.bass_utils import run_bass_kernel_spmd

    nc = bacc.Bacc("TRN2", target_bir_lowering=False, num_devices=1)
    arrays, args = {}, []
    for name, a in [(n, inputs[n]) for n in _INS] + [("positions", positions())]:
        a = np.ascontiguousarray(a)
        arrays[f"in_{name}"] = a
        args.append(nc.dram_tensor(f"in_{name}", a.shape, mybir.dt.from_np(a.dtype), kind="ExternalInput").ap())
    out = nc.dram_tensor("out", (B, SEQ, C), F32, kind="ExternalOutput").ap()
    layer(nc, *args, out)
    r = run_bass_kernel_spmd(nc, [arrays], core_ids=[0])
    return r.results[0]["out"]
```

```python
from contextlib import ExitStack

import concourse.bass as bass
from concourse import mybir

F32 = mybir.dt.float32
F16 = mybir.dt.float16
BF16 = mybir.dt.bfloat16
I32 = mybir.dt.int32
ALU = mybir.AluOpType
ACT = mybir.ActivationFunctionType
X = mybir.AxisListType.X

P = 128
B, SEQ = 8, 1024
C = 192
H, D = 12, 16
HID = 768
TB = SEQ // P
TH = TB // 2
NQ = TH * P
HALVES = 2 * B
KC = C // 2
HB = HID // P
KP = 2 * C // P
WB = 3 * C // KC
GH = 4
HG = H // GH
VE = D + 1
VW = H * VE + 2 * D - VE
GROUPS = 2 * H
UNITS = HG * TB
EPS = 1e-5
QN, QP = -8.0, 7.0
GELU_CLIP = 10.0
ROUND = 1.5 * 2.0 ** 23
MAGIC = float(0x5F3759DF)
QK_SCALE = 64.0
H_SCALE = 1024.0
W_TOP = 8192.0
O_DOWN = 64.0
SCORE_SCALE = D ** -0.5 / QK_SCALE ** 2

PLAN = """
;
Y0 ; Y1 w0 z0
Y2 Y3 F0 ; F1
F2 ; F3 G0
G1 ; G2 P0
G3 H0 ; H1
H2 ; H3 l0
W0 W1 W2 ;
W3 W4 W5 ; R0 m0 N0
;
;
; I0 I1
I2 I3 ; A0 A1
A2 A3 ; B0 X0 X1 B1 X2 X3 r0 B2 X4 X5 r1 B3 C0 C1 C2 C3 r2 r3 S0 n0
;
;
; n1 x0
; D0
E0 n2 ; D1
E1 n3 ; x1
; D2
E2 x2 ; D3
E3 x3 x4 ; x5
"""
JOB_KINDS = "ABCDEFGHIWXY"
UNIT_WORK = [[[(w[0], int(w[1])) for w in half.split()] for half in line.split(";")]
             for line in PLAN.strip().split("\n")]
UNIT_WORK += [[[], []]] * (UNITS - len(UNIT_WORK))
JOBS = [w for unit in UNIT_WORK for part in unit for w in part if w[0] in JOB_KINDS]
X_UNIT = next(u for u, unit in enumerate(UNIT_WORK) if ("X", 0) in unit[0] + unit[1])

FIRST_PLAN = """
P0 R0 N0 A0 A1 A2 A3 v0 P0' R0' N0' u0 B0 B1 r0 B2 r1 B3 r2 C0 C1 r3 C2 C3 S0
A0' A1' A2' A3' B0' B1' n0 n1 r0' r1' D0 E0 n2 B2' D1 E1 n3 B3' r2' C0' D2 E2 r3' D3 E3 S0'
n0' n1' C1' C2' C3' D0' E0' n2' D1' E1' n3' D2' E2' D3' E3'
"""
FIRST_WORK = [(w[0], int(w[1]), -1 if w[2:] else -2) for w in FIRST_PLAN.split()]

FIRST_GATHERED = range(3, 4)
GATHERED_BEFORE = {0: range(4, 8)}
GATHERED_AFTER = {0: range(8, 13), 1: range(13, HALVES)}

BANKS = 3
IN_TURN = [w for w in JOBS if w[0] not in "XB"]
LAG = {**dict.fromkeys("PNABCDE", 2), **dict.fromkeys("FGHIX", -1), "Y": -2, "W": 0}
PER_HALF = {**dict.fromkeys("ABCDEFGHIY", TH), **dict.fromkeys("XW", HB)}


def job_half(kind, s):
    return s + LAG[kind]


def job_runs(kind, s0):
    return s0 == 0 if kind == "W" else 0 <= job_half(kind, s0) < HALVES


def bank_of(job, s0):
    kind, t = job
    if s0 < 0:
        return jobs_of(s0).index((job, s0)) % BANKS
    return {"X": t % 2, "B": 2}[kind] if kind in "XB" else IN_TURN.index(job) % BANKS


def jobs_of(s0):
    if s0 < 0:
        return [((kind, t), s) for kind, t, s in FIRST_WORK if kind in JOB_KINDS]
    return [(job, s0) for job in JOBS if job_runs(job[0], s0)]


def job_before(job, s0):
    earlier = jobs_of(s0)
    earlier = earlier[:earlier.index((job, s0))]
    if s0 >= 0:
        earlier = jobs_of(s0 - 1) + earlier
    for other, s in reversed(earlier):
        if bank_of(other, s) == bank_of(job, s0):
            return other, s0 - s
    return None


def copied_by_act(kind, part, s0):
    return s0 < 0 and (kind in "ABCD" or (kind, part) == ("E", 1))


def layer(nc, x_tok, x_seg, tok_table, seg_table, w_qkv, w_proj, w1, b1, aw1, aa1, w2, b2, aw2, aa2,
          pos, out):
    ctx = ExitStack()
    with ctx:
        def sb(name, shape, dt=F32):
            return ctx.enter_context(nc.sbuf_tensor(name, shape, dt))

        def sem(name):
            return ctx.enter_context(nc.semaphore(name))

        h_all = sb("h_all", [P, B * TB * C])
        probs = sb("probs", [P, 2, GH, NQ])
        qT = sb("qT", [P, 2, H // 2, SEQ], F16)
        kA = sb("kA", [P, 2, H // 2, SEQ], F16)
        kB = sb("kB", [P, 2, H // 2, SEQ], F16)
        v_sb = sb("v_sb", [P, 2, TB, VW])
        parts = sb("parts", [P, TH, 2 * C], F16)
        partsT = sb("partsT", [P, TH, KP, P], F16)
        stack = sb("stack", [P, 2, 2, H, 4, D], F16)
        o_sb = sb("o_sb", [P, HG, NQ])
        gelu = sb("gelu", [P, HB, NQ])
        hq = sb("hq", [P, HB, NQ], BF16)
        sq = sb("sq", [P, 2, 2 * C])
        gelu_f = gelu[:].rearrange("p j n -> p (j n)")
        xf = gelu_f[:, 0:TH * C].rearrange("p (t c) -> p t c", c=C)
        y_sb = gelu_f[:, TH * C:2 * TH * C].rearrange("p (t c) -> p t c", c=C)
        hn = y_sb
        o_nat = xf
        qk = [parts[:, 2 * t:2 * t + 2].rearrange("p t c -> p (t c)").bitcast(F32) for t in range(2)]
        hq_tail = hq[:, HB // 2:HB].rearrange("p j n -> p (j n)").bitcast(F32)
        qk += [hq_tail[:, t * 2 * C:(t + 1) * 2 * C] for t in range(2)]
        start_f = probs[:].rearrange("p a g n -> p (a g n)")

        def qk_at(half0, t):
            at = (half0 * TH + t) * 2 * C
            return start_f[:, at:at + 2 * C] if half0 < 2 else qk[t]

        def squares_at(half0, t):
            at = (2 * TH + t % 2) * 2 * C
            return start_f[:, at:at + 2 * C] if half0 < 2 else sq[:, t % 2]

        xq = sq[:, 1].bitcast(BF16).rearrange("p (t c) -> p t c", c=C)
        stack_f = stack[:].rearrange("p s n h a d -> p (s n h a d)")
        xqT = stack_f[0:KC, 0:2 * NQ].bitcast(BF16).rearrange("p (k n) -> p k n", k=2)
        st, mv = sb("st", [P, 2, TH, 6]), sb("mv", [P, 2, TH, 2])
        vn, rn, wn = (sb(n, [P, 2, TH]) for n in ("vn", "rn", "wn"))
        vq, rq, wq_ = (sb(n, [P, TH, GROUPS]) for n in ("vq", "rq", "wq_"))
        ra2 = sb("ra2", [P, TH])
        rsum = sb("rsum", [P, H])
        gate_sb = sb("gate_sb", [P, 1])
        wh, wl = sb("wh", [P, KP, 3 * C], F16), sb("wl", [P, KP - 1, 3 * C], F16)
        wmean = sb("wmean", [P, KP, GROUPS])
        w_top, w_exp, w_scale = (sb(n, [P, 2]) for n in ("w_top", "w_exp", "w_scale"))
        w_back, one_down, proj_back = (sb(n, [P, 1]) for n in ("w_back", "one_down", "proj_back"))
        wph, wpl = sb("wph", [P, KP, C], F16), sb("wpl", [P, KP - 1, C], F16)
        w1T = sb("w1T", [KC, 2, HID], BF16)
        w2T = sb("w2T", [P, HB, C], BF16)
        a1, ia1, a2, ia2 = (sb(n, [P, 1]) for n in ("a1", "ia1", "a2", "ia2"))
        bound, qlo, qhi = (sb(n, [P, 1]) for n in ("bound", "qlo", "qhi"))
        aw1_sb, iaw1, s1_sb, b1_sb = (sb(n, [P, HB]) for n in ("aw1_sb", "iaw1", "s1_sb", "b1_sb"))
        aw2c, iaw2 = sb("aw2c", [KC, 2]), sb("iaw2", [KC, 2])
        s2_row, b2_row = sb("s2_row", [P, C]), sb("b2_row", [P, C])
        ident = sb("ident", [P, P])
        ident_h = sb("ident_h", [P, P], F16)
        ident_b = sb("ident_b", [P, P], BF16)
        idx = sb("idx", [P, 2, B * TB], I32)
        wq_nat = start_f[0:KC, 0:2 * WB * C].rearrange("p (r c) -> p r c", c=2 * C)
        wp_nat = start_f[0:KC, 2 * WB * C:(2 * WB + 4) * C].rearrange("p (r c) -> p r c", c=2 * C)
        aa1_in = start_f[:, (2 * WB + 4) * C:(2 * WB + 5) * C]
        aa2_in = start_f[:, (2 * WB + 5) * C:(2 * WB + 5) * C + HID]
        wT = qT[:].rearrange("p b i n -> p (b i n)").bitcast(F32)[:, 0:KP * 3 * C].rearrange("p (m c) -> p m c", m=KP)
        top_in = hq[0:KC].rearrange("p j n -> p (j n)").bitcast(F32)
        tops = WB + 2
        row_top, row_low = top_in[:, 0:tops], top_in[:, tops:2 * tops]
        top_row = top_in[:, 2 * tops:2 * tops + 2 * P].rearrange("p (w n) -> p w n", w=2)
        hq_f = hq[:].rearrange("p j n -> p (j n)").bitcast(F32)
        idx_in, idx_f = (hq_f[:, n * 2 * B * TB:(n + 1) * 2 * B * TB].rearrange("p (w b j) -> p w b j", w=2, b=B)
                         for n in (3, 4))
        idx_in = idx_in.bitcast(I32)
        qT_f = qT[:].rearrange("p b i n -> p (b i n)").bitcast(F32)[:, H // 4 * SEQ:H // 2 * SEQ]
        w1_nat = qT_f[:, 0:HB * C].rearrange("p (j c) -> p j c", c=C)
        w2_nat = qT_f[0:KC, HB * C:HB * C + 2 * HID].rearrange("p (r h) -> p r h", h=HID)

        ps_s = ctx.enter_context(nc.psum_tensor("ps_s", [P, GH, NQ], F32))
        ps_o = ctx.enter_context(nc.psum_tensor("ps_o", [P, NQ], F32))
        ps_j = ctx.enter_context(nc.psum_tensor("ps_j", [P, BANKS, 512], F32))

        idx_loaded, w_loaded, aw_loaded = sem("idx_loaded"), sem("w_loaded"), sem("aw_loaded")
        pos_loaded, ffn_loaded = sem("pos_loaded"), sem("ffn_loaded")
        seg_added, tok_added = ([sem(f"{n}{i}") for i in range(2)] for n in ("seg_added", "tok_added"))
        idx_ready, ident_ready = sem("idx_ready"), sem("ident_ready")
        zero_halves = [sem(f"zero_halves{b}") for b in range(2)]
        pool_step, dve_step = sem("pool_step"), sem("dve_step")
        weights_ready, proj_ready = sem("weights_ready"), sem("proj_ready")
        top_ready, top_mm = sem("top_ready"), sem("top_mm")
        ones_written, ffn_quantised = sem("ones_written"), sem("ffn_quantised")
        hn_ready, stack_ready, xq_ready, hq_ready = (
            sem(n) for n in ("hn_ready", "stack_ready", "xq_ready", "hq_ready"))
        scores_mm, exp_done, heads_mm, heads_out = (
            sem(n) for n in ("scores_mm", "exp_done", "heads_mm", "heads_out"))
        squared, summed, high_ready = sem("squared"), sem("summed"), sem("high_ready")
        out_ready, stored = sem("out_ready"), sem("stored")
        job_mm = {k: sem(f"{k}_mm") for k in PER_HALF}
        job_out = {k: sem(f"{k}_out") for k in PER_HALF}
        E_odd_out = sem("E_odd_out")

        def out_sems(kind):
            return [job_out["E"], E_odd_out] if kind == "E" else [job_out[kind]]

        def nth(half, t, per):
            return half * per + (t + 1)

        def h_tile(half, t):
            return h_all[:, bass.ds(half * (TH * C) + t * C, C)]

        def bank(job, s0):
            return ps_j[:, bank_of(job, s0), :]

        def bank16(job, s0, dt):
            return bank(job, s0).bitcast(dt)

        def attends(s0):
            return 0 <= s0 < HALVES

        def copies(s0, s, kind, t):
            if kind not in "ABCDEGI":
                return []
            half0 = job_half(kind, s0)
            tile, par = half0 % 2 * TH + t, half0 // 2 % 2
            ps, ps16 = bank((kind, t), s0), bank16((kind, t), s0, BF16 if kind == "I" else F16)
            three = lambda a: a[:, 0:KP * P].rearrange("p (m n) -> p m n", m=KP)
            two = lambda a: a[0:KC, 0:2 * P].rearrange("p (k n) -> p k n", k=2)
            six = lambda a: a[:, 0:H // 2 * P].rearrange("p (i n) -> p i n", n=P)
            here = slice(tile * P, (tile + 1) * P)
            if kind in "AG":
                return [(partsT[:, t], three(ps16))]
            if kind == "B":
                return [(qk_at(half0, t), ps[:, 0:2 * C])]
            if kind == "C":
                return [(v_sb[:, par, tile, 0:H * VE].rearrange("p (h e) -> p h e", e=VE)[:, :, 0:D],
                         ps[:, 0:C].rearrange("p (h d) -> p h d", d=D))]
            if kind == "D":
                return [(qT[:, par, :, here], six(ps16))]
            if kind == "E":
                return [(kA[0:P // 2, par, :, here], six(ps16[0:P // 2])),
                        (kB[P // 2:P, par, :, here], six(ps16[P // 2:P]))]
            if kind == "I":
                return [(xqT[:, :, t * P:(t + 1) * P], two(ps16))]

        def stack_parts(t):
            for n, (high, low) in enumerate(((slice(0, 2), slice(2, 4)), (slice(0, 4, 2), slice(1, 4, 2)))):
                src = sq[:, t % 2, n * C:(n + 1) * C].rearrange("p (h d) -> p h d", d=D)
                src = src.unsqueeze(2).broadcast_to([P, H, 2, D])
                yield stack[:, t % 2, n, :, high, :], stack[:, t % 2, n, :, low, :], src

        def halfsteps(eng, one):
            for s in range(2):
                one(s, s, s // 2)
            with eng.Fori(0, (B - 2) // 2) as turn:
                for k in range(4):
                    one(2 + k, turn * 4 + (2 + k), turn * 2 + (1 + k // 2))
            for s in range(HALVES - 2, HALVES + 2):
                one(s, s, s // 2)

        block = ctx.enter_context(nc.Block())

        @block.sync
        def _(sp):
            sp.dma_start(idx_in[:, 0], x_tok.rearrange("b (p j) -> p b j", j=TB)).then_inc(idx_loaded, 16)
            sp.dma_start(idx_in[:, 1], x_seg.rearrange("b (p j) -> p b j", j=TB)).then_inc(idx_loaded, 16)
            pos_v = pos.rearrange("(p j) c -> p (j c)", j=TB)

            def load_pos(b):
                sp.dma_start(h_all[:, b * TB * C:(b + 1) * TB * C], pos_v).then_inc(pos_loaded, 16)
                sp.wait_ge(pos_loaded, 16 * (b + 1))

            load_pos(0)
            for nat, w in ((wq_nat, w_qkv), (wp_nat, w_proj)):
                for n in range(2):
                    sp.dma_start(nat[:, :, n * C:(n + 1) * C],
                                 w.rearrange("(r p) c -> p r c", p=KC)).then_inc(w_loaded, 16)
            sp.dma_start(w1_nat, w1.rearrange("(p j) c -> p j c", j=HB)).then_inc(ffn_loaded, 16)
            sp.dma_start(w2_nat, w2.rearrange("(p r) h -> p r h", r=2)).then_inc(ffn_loaded, 16)
            for b in range(1, B):
                load_pos(b)

            def one(s0, s, b):
                if not job_runs("Y", s0):
                    return
                y = job_half("Y", s)
                sp.wait_ge(out_ready, nth(y, 0, 1))
                sp.dma_start(out_rows[:, bass.ds(b - 1, 1), s0 % 2 * TH * C:(s0 % 2 + 1) * TH * C],
                             h_all[:, bass.ds(y * (TH * C), TH * C)]).then_inc(stored, 16)

            out_rows = out.rearrange("b (p j) c -> p b (j c)", j=TB)
            halfsteps(sp, one)
            sp.wait_ge(stored, 16 * HALVES)

        @block.gpsimd
        def _(pool):
            def gather(table, which, half, done):
                for j in range(TH):
                    t = half * TH + j
                    nc.gpsimd.indirect_dma_start(
                        out=h_all[:, t * C:(t + 1) * C], out_offset=None, in_=table,
                        in_offset=bass.IndirectOffsetOnAxis(ap=idx[:, which, t:t + 1], axis=0),
                        compute_op=ALU.add).then_inc(done, 16)

            for m in (ident, ident_h, ident_b):
                nc.gpsimd.memset(m[:], 0.0).then_inc(pool_step, 1)
            for n, m in enumerate((ident, ident_h, ident_b)):
                pool.wait_ge(pool_step, n + 1)
                nc.gpsimd.affine_select(out=m[:], in_=m[:], compare_op=ALU.not_equal, fill=1.0, base=0,
                                        pattern=[[-1, P]], channel_multiplier=1).then_inc(ident_ready, 1)

            def add_segments(half):
                pool.wait_ge(pos_loaded, 16 * (half // 2 + 1))
                gather(seg_table, 1, half, seg_added[half % 2])

            def add_tokens(half):
                pool.wait_ge(seg_added[half % 2], 16 * TH * (half // 2 + 1))
                if half >= 2:
                    pool.wait_ge(tok_added[half % 2], 16 * TH * (half // 2))
                gather(tok_table, 0, half, tok_added[half % 2])

            pool.wait_ge(idx_ready, 1)
            for half in range(2):
                add_segments(half)
            pool.wait_ge(idx_ready, 2)
            for half in range(2):
                add_tokens(half)
            add_segments(2)
            pool.wait_ge(ident_ready, 3)
            nc.gpsimd.memset(kA[P // 2:P, 0].bitcast(F32), 0.0).then_inc(zero_halves[0], 1)
            pool.wait_ge(zero_halves[0], 1)
            nc.gpsimd.memset(kB[0:P // 2, 0].bitcast(F32), 0.0).then_inc(zero_halves[0], 1)
            add_tokens(2)

            def gather_halves(halves):
                if halves:
                    add_segments(halves[0])
                for half in halves:
                    if half + 1 in halves:
                        add_segments(half + 1)
                    add_tokens(half)

            gather_halves(FIRST_GATHERED)

            def square(s0, s):
                if not job_runs("B", s0):
                    return
                half = job_half("B", s)
                for t in range(TH):
                    pool.wait_ge(job_out["B"], nth(half, t, TH))
                    if job_half("B", s0) or t >= 2:
                        pool.wait_ge(summed, half * TH + (t - 1))
                    nc.gpsimd.tensor_tensor(sq[:, t % 2], qk[t], qk[t], ALU.mult).then_inc(squared, 1)

            def split_low(s0, s):
                if not job_runs("D", s0):
                    return
                for t in range(TH):
                    pool.wait_ge(high_ready, nth(job_half("D", s), t, TH))
                    for high, low, src in stack_parts(t):
                        last = nc.gpsimd.tensor_tensor(low, src, high, ALU.subtract)
                    last.then_inc(stack_ready, 1)

            def add_result(s0, s):
                if not job_runs("Y", s0):
                    return
                y = job_half("Y", s)
                pool.wait_ge(job_out["Y"], nth(y, TH - 1, TH))
                nc.gpsimd.tensor_tensor(y_sb, y_sb, b2_row[:].unsqueeze(1).broadcast_to([P, TH, C]),
                                        ALU.add).then_inc(pool_step, 1)
                pool.wait_ge(pool_step, y + 4)
                hv = h_all[:, bass.ds(y * (TH * C), TH * C)]
                nc.gpsimd.tensor_tensor(hv, hv, gelu_f[:, TH * C:2 * TH * C],
                                        ALU.add).then_inc(out_ready, 1)

            def one(s0, s, b):
                gather_halves(GATHERED_BEFORE.get(s0, ()))
                add_result(s0, s)
                square(s0, s)
                split_low(s0, s)
                gather_halves(GATHERED_AFTER.get(s0, ()))

            for s in (-2, -1):
                split_low(s, s)
            halfsteps(pool, one)

        @block.scalar
        def _(act):
            act.dma_start(aa1_in, aa1.unsqueeze(0).broadcast_to([P, C])).then_inc(aw_loaded, 16)
            act.dma_start(aa2_in, aa2.unsqueeze(0).broadcast_to([P, HID])).then_inc(aw_loaded, 16)
            act.dma_start(aw1_sb[:], aw1.rearrange("(p j) -> p j", j=HB)).then_inc(aw_loaded, 16)
            act.dma_start(b1_sb[:], b1.rearrange("(p j) -> p j", j=HB)).then_inc(aw_loaded, 16)
            act.dma_start(aw2c[:], aw2.rearrange("(p r) -> p r", r=2)).then_inc(aw_loaded, 16)
            act.dma_start(s2_row[:], aw2.unsqueeze(0).broadcast_to([P, C])).then_inc(aw_loaded, 16)
            act.dma_start(b2_row[:], b2.unsqueeze(0).broadcast_to([P, C])).then_inc(aw_loaded, 16)
            act.wait_ge(weights_ready, 1)

            def copy_out(s0, s, kind, t):
                for part, (dst, src) in enumerate(copies(s0, s, kind, t)):
                    if not copied_by_act(kind, part, s0):
                        continue
                    half = job_half(kind, s)
                    if kind == "C" and t == 0:
                        act.wait_ge(ones_written, 2)
                    act.wait_ge(job_mm[kind], nth(half, t, TH))
                    scale = w_back[:] if kind in "BC" else 1.0
                    nc.scalar.activation(dst, src, ACT.Copy, scale=scale).then_inc(out_sems(kind)[part], 1)

            def square(s0, s, t):
                half = job_half("B", s)
                act.wait_ge(job_out["B"], nth(half, t, TH))
                if job_half("B", s0) or t >= 2:
                    act.wait_ge(summed, half * TH + (t - 1))
                nc.scalar.activation(squares_at(half, t), qk_at(half, t), ACT.Square).then_inc(squared, 1)

            def gelu_out(s0, s, j):
                half = job_half("X", s)
                act.wait_ge(job_mm["X"], nth(half, j, HB))
                if j == 0 and job_runs("Y", s0):
                    act.wait_ge(out_ready, nth(job_half("Y", s), 0, 1))
                nc.scalar.activation(gelu[:, j], bank(("X", j), s0), ACT.Gelu, bias=b1_sb[:, j:j + 1],
                                     scale=s1_sb[:, j:j + 1]).then_inc(job_out["X"], 1)

            def exps(s0, s, u, pair):
                act.wait_ge(scores_mm, 2 * UNITS * s + (2 * u + pair + 1))
                nc.scalar.activation(probs[:, u % 2, 2 * pair:2 * pair + 2], ps_s[:, 2 * pair:2 * pair + 2],
                                     ACT.Exp, scale=SCORE_SCALE).then_inc(exp_done, 1)

            def one(s0, s, b):
                for u in range(UNITS):
                    if u == X_UNIT and job_runs("X", s0):
                        for j in range(HB):
                            gelu_out(s0, s, j)
                    for pair in range(2):
                        if attends(s0):
                            exps(s0, s, u, pair)

            for kind, t, s in FIRST_WORK:
                copy_out(s, s, kind, t)
                if kind == "B":
                    square(s, s, t)
            halfsteps(act, one)

        @block.vector
        def _(dve):
            steps = {"done": 0, "turns": 0}

            def link(ins):
                steps["done"] += 1
                ins.then_inc(dve_step, 1)
                dve.wait_ge(dve_step, steps["turns"] + steps["done"])

            ts = nc.vector.tensor_scalar
            tt = nc.vector.tensor_tensor
            stt = nc.vector.scalar_tensor_tensor

            def rsqrt(y, v, w):
                link(ts(w.bitcast(I32), v.bitcast(I32), 1, None, ALU.logical_shift_right))
                link(ts(y.bitcast(I32), w.bitcast(I32), -1.0, MAGIC, ALU.mult, ALU.add))
                for _ in range(3):
                    link(stt(out=w, in0=y, scalar=-0.5, in1=y, op0=ALU.mult, op1=ALU.mult))
                    link(tt(w, w, v, ALU.mult))
                    link(stt(out=y, in0=w, scalar=1.5, in1=y, op0=ALU.add, op1=ALU.mult))

            def gate():
                nc.vector.memset(gate_sb[:], 0.0)

            def norm_stats(which, half):
                gate()
                for t in range(TH):
                    last = nc.vector.bn_stats(st[:, which, t], h_tile(half, t))
                link(last)
                gate()
                for t in range(TH):
                    last = nc.vector.bn_aggr(mv[:, which, t], st[:, which, t])
                link(last)
                scale = 1.0 if which else H_SCALE ** -2
                link(ts(vn[:, which], mv[:, which, :, 1], EPS, scale, ALU.add, ALU.mult))

            def norm_roots(s0):
                lo = 0 if job_runs("P", s0) else 1
                hi = 2 if job_runs("H", s0) else 1
                if lo < hi:
                    rsqrt(rn[:, lo:hi], vn[:, lo:hi], wn[:, lo:hi])

            def first_norm(s0, s):
                half = job_half("N", s)
                if job_runs("Y", s0):
                    dve.wait_ge(out_ready, nth(job_half("Y", s), 0, 1))
                if s0 == -1:
                    dve.wait_ge(job_mm["A"], TH)
                for t in range(TH):
                    last = ts(hn[:, t], h_tile(half, t), mv[:, 0, t, 0:1], rn[:, 0, t:t + 1],
                              ALU.subtract, ALU.mult)
                link(last)
                link(nc.vector.tensor_copy(parts[:, :, 0:C], hn))
                tt(parts[:, :, C:2 * C], hn, parts[:, :, 0:C], ALU.subtract).then_inc(hn_ready, 1)

            def quantise(dst, src, tmp, lo, hi):
                link(ts(tmp, src, lo, hi, ALU.max, ALU.min))
                return ts(dst, tmp, ROUND, -ROUND, ALU.add, ALU.add)

            def quantise_ffn():
                dve.wait_ge(ffn_loaded, 16 * 2)
                for nat, ia, n in ((w1_nat, iaw1, HB), (w2_nat, iaw2, 2)):
                    for j in range(n):
                        last = ts(nat[:, j], nat[:, j], ia[:, j:j + 1], None, ALU.mult)
                    link(last)
                    quantise(nat, nat, nat, QN, QP).then_inc(ffn_quantised, 1)

            def squares_sum(s0, s, t):
                half = job_half("B", s)
                dve.wait_ge(squared, nth(half, t, TH))
                nc.vector.tensor_reduce(vq[:, t], squares_at(job_half("B", s0), t).rearrange("p (g d) -> p g d", d=D),
                                        X, ALU.add).then_inc(summed, 1)

            def qk_roots(s0, s):
                dve.wait_ge(summed, nth(job_half("B", s), TH - 1, TH))
                link(ts(vq[:], vq[:], 1.0 / (D * QK_SCALE ** 2), EPS / QK_SCALE ** 2, ALU.mult, ALU.add))
                rsqrt(rq[:], vq[:], wq_[:])

            def split_qk(s0, s, t):
                half, h0 = job_half("D", s), job_half("D", s0)
                g = lambda a: a.rearrange("p (g d) -> p g d", d=D)
                if TH * h0 + t >= 2:
                    dve.wait_ge(stack_ready, half * TH + (t - 1))
                link(tt(g(sq[:, t % 2]), g(qk_at(h0, t)), rq[:, t, 0:GROUPS].unsqueeze(2).broadcast_to([P, GROUPS, D]), ALU.mult))
                if t == 0 and job_runs("X", s0):
                    dve.wait_ge(job_mm["X"], nth(job_half("X", s), HB - 1, HB))
                if TH * h0 + t >= 2:
                    dve.wait_ge(job_mm["E"], half * TH + (t - 1))
                for high, _, src in stack_parts(t):
                    last = nc.vector.tensor_copy(high, src)
                last.then_inc(high_ready, 1)

            def head_outputs(s0, s, group):
                dve.wait_ge(heads_mm, UNITS * s + TB * (group + 1))
                nc.vector.tensor_copy(o_sb[:, group], ps_o[:]).then_inc(heads_out, 1)

            def second_norm(s0, s):
                half = job_half("I", s)
                link(ts(ra2[:], rn[:, 1], ia1[:], None, ALU.mult))
                for t in range(TH):
                    last = ts(xf[:, t], h_tile(half, t), mv[:, 1, t, 0:1], ra2[:, t:t + 1],
                              ALU.subtract, ALU.mult)
                link(last)
                quantise(xq, xf, xf, QN, QP).then_inc(xq_ready, 1)

            def quantise_gelu(s0, s, t):
                dve.wait_ge(job_out["X"], nth(job_half("X", s), t, HB))
                link(ts(gelu[:, t], gelu[:, t], ia2[:], qlo[:], ALU.mult, ALU.max))
                link(ts(gelu[:, t], gelu[:, t], qhi[:], ROUND, ALU.min, ALU.add))
                ts(hq[:, t], gelu[:, t], ROUND, None, ALU.subtract).then_inc(hq_ready, 1)

            def job_result(s0, s, kind, t):
                if not job_runs(kind, s0):
                    return
                half, h0 = job_half(kind, s), job_half(kind, s0)
                job = (kind, t)
                ps = bank(job, s0)
                for part, (dst, src) in enumerate(copies(s0, s, kind, t)):
                    if copied_by_act(kind, part, s0):
                        continue
                    dve.wait_ge(job_mm[kind], nth(half, t, TH))
                    if kind in "BC":
                        last = ts(dst, src, w_back[:], None, ALU.mult)
                    else:
                        last = nc.vector.tensor_copy(dst, src)
                    last.then_inc(out_sems(kind)[part], 1)
                if kind == "W":
                    dve.wait_ge(job_mm["W"], t + 1)
                    if t < 3:
                        nc.vector.tensor_copy(
                            w1T[:, :, 2 * t * P:2 * (t + 1) * P],
                            ps[0:KC, :].rearrange("p (k n) -> p k n", k=2)).then_inc(job_out["W"], 1)
                    else:
                        nc.vector.tensor_copy(
                            w2T[:, 2 * (t - 3):2 * (t - 2)].rearrange("p j (c r) -> p j c r", r=2),
                            ps[:, 0:2 * C].rearrange("p (j r c) -> p j c r", j=2, r=2)).then_inc(job_out["W"], 1)
                if kind == "F":
                    dve.wait_ge(job_mm["F"], nth(half, t, TH))
                    heads = ps[:, 0:H * 2 * D].rearrange("p (h e) -> p h e", e=2 * D)
                    if h0 or t:
                        dve.wait_ge(job_out["F"], half * TH + t)
                    link(nc.vector.reciprocal(rsum[:], heads[:, :, D]))
                    link(tt(o_nat[:, t].rearrange("p (h d) -> p h d", d=D), heads[:, :, 0:D],
                            rsum[:].unsqueeze(2).broadcast_to([P, H, D]), ALU.mult))
                    link(nc.vector.tensor_copy(parts[:, t, 0:C], o_nat[:, t]))
                    tt(parts[:, t, C:2 * C], o_nat[:, t], parts[:, t, 0:C], ALU.subtract).then_inc(job_out["F"], 1)
                if kind == "H":
                    dve.wait_ge(job_mm["H"], nth(half, t, TH))
                    stt(out=h_tile(half, t), in0=ps[:, 0:C], scalar=proj_back[:], in1=h_tile(half, t),
                        op0=ALU.mult, op1=ALU.add).then_inc(job_out["H"], 1)
                    if t == TH - 1:
                        dve.wait_ge(job_out["H"], nth(half, t, TH))
                if kind == "Y":
                    dve.wait_ge(job_mm["Y"], nth(half, t, TH))
                    if h0 >= 1 and t == 0:
                        dve.wait_ge(out_ready, nth(half - 1, 0, 1))
                    tt(y_sb[:, t], ps[:, 0:C], s2_row[:], ALU.mult).then_inc(job_out["Y"], 1)

            def start():
                nc.vector.memset(v_sb[:], 1.0).then_inc(ones_written, 1)
                dve.wait_ge(idx_loaded, 32)
                for w, rows in ((1, seg_table.shape[0]), (0, tok_table.shape[0])):
                    link(ts(idx_f[:, w], idx_in[:, w], 0.0, float(rows), ALU.is_lt, ALU.mult))
                    link(tt(idx_f[:, w], idx_f[:, w], idx_in[:, w], ALU.add))
                    ts(idx[:, w], idx_f[:, w].rearrange("p b j -> p (b j)"), 0.0, float(rows - 1),
                       ALU.max, ALU.min).then_inc(idx_ready, 1)
                dve.wait_ge(aw_loaded, 16 * 7)
                for a, ia, src, n in ((a1, ia1, aa1_in, C), (a2, ia2, aa2_in, HID)):
                    link(nc.vector.tensor_reduce(a[:], src, X, ALU.add))
                    link(ts(a[:], a[:], 1.0 / n, None, ALU.mult))
                    link(nc.vector.reciprocal(ia[:], a[:]))
                link(ts(bound[:], ia2[:], -GELU_CLIP, None, ALU.mult))
                link(stt(out=bound[:], in0=ia2[:], scalar=GELU_CLIP, in1=bound[:], op0=ALU.mult, op1=ALU.max))
                link(ts(qhi[:], bound[:], QP, None, ALU.min))
                link(ts(qlo[:], bound[:], -1.0, QN, ALU.mult, ALU.max))
                link(ts(s1_sb[:], aw1_sb[:], a1[:], None, ALU.mult))
                link(ts(s2_row[:], s2_row[:], a2[:], None, ALU.mult))
                link(nc.vector.reciprocal(iaw1[:], aw1_sb[:]))
                link(nc.vector.reciprocal(iaw2[:], aw2c[:]))
                dve.wait_ge(w_loaded, 16 * 4)
                for dst, op in ((row_top, ALU.max), (row_low, ALU.min)):
                    nc.vector.tensor_reduce(dst[:, 0:WB], wq_nat[:, :, 0:C], X, op)
                    last = nc.vector.tensor_reduce(dst[:, WB:tops], wp_nat[:, :, 0:C], X, op)
                link(last)
                link(stt(out=row_top, in0=row_low, scalar=-1.0, in1=row_top, op0=ALU.mult, op1=ALU.max))
                nc.vector.tensor_reduce(w_top[0:KC, 0:1], row_top[:, 0:WB], X, ALU.max)
                link(nc.vector.tensor_reduce(w_top[0:KC, 1:2], row_top[:, WB:tops], X, ALU.max))
                nc.vector.tensor_copy(top_row, w_top[0:KC].unsqueeze(2).broadcast_to([KC, 2, P])).then_inc(top_ready, 1)
                dve.wait_ge(top_mm, 1)
                link(nc.vector.tensor_reduce(w_top[:], ps_s[:, 3, 0:2 * KC].rearrange("p (w n) -> p w n", w=2), X, ALU.max))
                link(ts(w_top[:], w_top[:], 2.0 ** -100, None, ALU.max))
                link(ts(w_exp[:].bitcast(I32), w_top[:].bitcast(I32), 23, None, ALU.logical_shift_right))
                link(ts(w_top[:].bitcast(I32), w_exp[:].bitcast(I32), 23, None, ALU.logical_shift_left))
                link(nc.vector.reciprocal(w_scale[:], w_top[:]))
                link(ts(w_scale[:], w_scale[:], W_TOP, None, ALU.mult))
                ts(w_back[:], w_top[:, 0:1], 1.0 / (W_TOP * H_SCALE), None, ALU.mult)
                for m in range(KP):
                    nc.vector.tensor_copy(wT[:, m, 0:2 * C], ps_j[:, m, 0:2 * C])
                link(nc.vector.tensor_copy(wT[:, :, 2 * C:3 * C], ps_s[:, 0:KP, 0:C]))
                g = wT[:, :, 0:2 * C].rearrange("p m (g d) -> p m g d", d=D)
                link(nc.vector.tensor_reduce(wmean[:], g, X, ALU.add))
                link(ts(wmean[:], wmean[:], -1.0 / D, None, ALU.mult))
                for m in range(KP):
                    g = wT[:, m, 0:2 * C].rearrange("p (g d) -> p g d", d=D)
                    last = tt(g, g, wmean[:, m].unsqueeze(2).broadcast_to([P, GROUPS, D]), ALU.add)
                link(last)
                link(ts(wT, wT, w_scale[:, 0:1], None, ALU.mult))

            def split_weights():
                link(nc.vector.tensor_copy(wh[:], wT))
                tt(wl[:], wT[:, 0:KP - 1], wh[:, 0:KP - 1], ALU.subtract).then_inc(weights_ready, 1)
                link(ts(one_down[:], w_top[:, 0:1], O_DOWN / W_TOP, None, ALU.mult))
                dve.wait_ge(ones_written, 1)
                for b in range(2):
                    ones = v_sb[:, b, :, 0:H * VE].rearrange("p t (h e) -> p t h e", e=VE)[:, :, :, D]
                    last = ts(ones, ones, one_down[:], None, ALU.mult)
                last.then_inc(ones_written, 1)

            def split_proj():
                link(ts(proj_back[:], w_top[:, 1:2], one_down[:], 1.0 / W_TOP, ALU.mult, ALU.mult))
                sources = (ps_o[:, 0:C], ps_o[:, C:2 * C], ps_s[:, 3, 2 * KC:2 * KC + C])
                for m in range(KP):
                    last = ts(wph[:, m], sources[m], w_scale[:, 1:2], None, ALU.mult)
                link(last)
                for m in range(KP - 1):
                    last = stt(out=wpl[:, m], in0=sources[m], scalar=w_scale[:, 1:2], in1=wph[:, m],
                               op0=ALU.mult, op1=ALU.subtract)
                last.then_inc(proj_ready, 1)

            def work(s0, s, kind, t):
                if kind == "P" and job_runs("P", s0):
                    p = job_half("P", s)
                    dve.wait_ge(tok_added[s0 % 2], (p - s0 % 2 + 2) * (TH * 8))
                    norm_stats(0, p)
                elif kind == "l" and job_runs("H", s0):
                    norm_stats(1, job_half("H", s))
                elif kind == "R":
                    norm_roots(s0)
                elif kind == "N" and job_runs("N", s0):
                    first_norm(s0, s)
                elif kind == "m" and job_runs("I", s0):
                    second_norm(s0, s)
                elif kind == "r" and job_runs("B", s0):
                    squares_sum(s0, s, t)
                elif kind == "S" and job_runs("B", s0):
                    qk_roots(s0, s)
                elif kind == "n" and job_runs("D", s0):
                    split_qk(s0, s, t)
                elif kind == "x" and job_runs("X", s0):
                    quantise_gelu(s0, s, t)
                elif kind == "v":
                    split_weights()
                elif kind == "u":
                    split_proj()
                elif kind == "z" and s0 == 0:
                    nc.vector.memset(kA[P // 2:P, 1].bitcast(F32), 0.0).then_inc(zero_halves[1], 1)
                    nc.vector.memset(kB[0:P // 2, 1].bitcast(F32), 0.0).then_inc(zero_halves[1], 1)
                elif kind == "w" and s0 == 0:
                    quantise_ffn()
                elif kind in job_out:
                    job_result(s0, s, kind, t)

            def one(s0, s):
                for u in range(UNITS):
                    for n, unit_part in enumerate(UNIT_WORK[u]):
                        if n == 1 and u % TB == 0:
                            if u == 0 and attends(s0 - 1):
                                head_outputs(s0 - 1, s - 1, HG - 1)
                            elif u and attends(s0):
                                head_outputs(s0, s, u // TB - 1)
                        for kind, t in unit_part:
                            work(s0, s, kind, t)

            start()
            for kind, t, s in FIRST_WORK:
                work(s, s, kind, t)
            for s in range(2):
                one(s, s)
            before = steps["done"]
            with dve.Fori(0, (B - 2) // 2) as turn:
                steps["turns"] = turn * LINKS_PER_TURN
                for k in range(4):
                    one(2 + k, turn * 4 + (2 + k))
            assert steps["done"] - before == LINKS_PER_TURN, steps["done"] - before
            steps["turns"] = ((B - 2) // 2 - 1) * LINKS_PER_TURN
            for s in range(HALVES - 2, HALVES + 2):
                one(s, s)

        @block.tensor
        def _(pe):
            mm = nc.tensor.matmul

            def start():
                pe.wait_ge(ident_ready, 3)
                pe.wait_ge(w_loaded, 16 * 4)
                for m in range(KP):
                    for r in range(WB):
                        dst = ps_j[:, m, r * KC:(r + 1) * KC] if r < 4 else ps_s[:, m, (r - 4) * KC:(r - 3) * KC]
                        nc.tensor.transpose(dst, wq_nat[:, r, m * P:(m + 1) * P], ident[0:KC, 0:KC])
                    for r in range(2):
                        at = r * KC
                        dst = ps_o[:, m * C + at:m * C + at + KC] if m < 2 else ps_s[:, 3, 2 * KC + at:3 * KC + at]
                        nc.tensor.transpose(dst, wp_nat[:, r, m * P:(m + 1) * P], ident[0:KC, 0:KC])
                pe.wait_ge(top_ready, 1)
                for w in range(2):
                    last = nc.tensor.transpose(ps_s[:, 3, w * KC:(w + 1) * KC], top_row[:, w], ident[0:KC, 0:KC])
                last.then_inc(top_mm, 1)

            def scores(s0, s, u):
                par, nh = s0 // 2 % 2, s0 % 2
                group, m = divmod(u, TB)
                if u == 0 and nh == 0:
                    if s0 <= 2:
                        pe.wait_ge(zero_halves[par], 2)
                    pe.wait_ge(job_out["D"], (s + 2) * TH)
                    pe.wait_ge(job_out["E"], (s + 2) * TH)
                    pe.wait_ge(E_odd_out, (s + 2) * TH)
                for j in range(GH):
                    if j % 2 == 0 and (u or attends(s0 - 1)):
                        pe.wait_ge(exp_done, 2 * UNITS * s + (2 * u - 1 + j // 2))
                    head = GH * group + j
                    k = kA if head % 2 == 0 else kB
                    last = mm(ps_s[:, j], k[:, par, head // 2, m * P:(m + 1) * P],
                              qT[:, par, head // 2, nh * NQ:(nh + 1) * NQ], start=True, stop=True)
                    if j % 2:
                        last.then_inc(scores_mm, 1)

            def heads(s0, s, u):
                par = s0 // 2 % 2
                group, m = divmod(u, TB)
                if u == 0 and s0 % 2 == 0:
                    pe.wait_ge(job_out["C"], (s + 2) * TH)
                if m == 0 and (group or attends(s0 - 1)):
                    pe.wait_ge(heads_out, HG * s + group)
                pe.wait_ge(exp_done, 2 * UNITS * s + (2 * u + 2))
                for j in range(GH):
                    last = mm(ps_o[32 * j:32 * j + 2 * D, :], v_sb[:, par, m, (GH * group + j) * VE:(GH * group + j) * VE + 2 * D],
                              probs[:, u % 2, j], start=(m == 0), stop=(m == TB - 1))
                last.then_inc(heads_mm, 1)

            def job(s0, s, kind, t):
                if not job_runs(kind, s0):
                    return
                half, h0 = job_half(kind, s), job_half(kind, s0)
                prior = job_before((kind, t), s0)
                if prior:
                    (pk, pt), back = prior
                    for out_sem in out_sems(pk):
                        pe.wait_ge(out_sem, nth(job_half(pk, s - back), pt, PER_HALF[pk]))
                ps = bank((kind, t), s0)
                if kind == "A":
                    if t == 0:
                        pe.wait_ge(hn_ready, nth(half, 0, 1))
                if kind == "B":
                    if (s0, t) == (-2, 0):
                        pe.wait_ge(weights_ready, 1)
                    pe.wait_ge(job_out["A"], nth(half, t, TH))
                if kind == "H":
                    if (s0, t) == (1, 0):
                        pe.wait_ge(proj_ready, 1)
                    pe.wait_ge(job_out["G"], nth(half, t, TH))
                if kind in "BCH":
                    lo, hi = {"B": (0, 2 * C), "C": (2 * C, 3 * C), "H": (0, C)}[kind]
                    high, low = (wph[:], wpl[:]) if kind == "H" else (wh[:, :, lo:hi], wl[:, :, lo:hi])
                    passes = [(m, high[:, m]) for m in range(KP)] + [(m, low[:, m]) for m in range(KP - 1)]
                    for n, (m, w) in enumerate(passes):
                        last = mm(ps[:, 0:hi - lo], partsT[:, t, m], w, start=(n == 0), stop=(n == len(passes) - 1))
                if kind in "DE":
                    pe.wait_ge(stack_ready, nth(half, t, TH))
                    for i in range(H // 2):
                        src = stack[:, t % 2, "DE".index(kind), 2 * i:2 * i + 2].rearrange("p h a d -> p (h a d)")
                        last = nc.tensor.transpose(bank16((kind, t), s0, F16)[:, i * P:(i + 1) * P], src, ident_h[:])
                if kind == "F":
                    if t == 0:
                        pe.wait_ge(heads_out, nth(half, HG - 1, HG))
                    for g in range(HG):
                        last = nc.tensor.transpose(ps[:, g * P:(g + 1) * P], o_sb[:, g, t * P:(t + 1) * P], ident[:])
                if kind == "G":
                    pe.wait_ge(job_out["F"], nth(half, t, TH))
                if kind in "AG":
                    for m in range(KP):
                        last = nc.tensor.transpose(bank16((kind, t), s0, F16)[:, m * P:(m + 1) * P],
                                                   parts[:, t, m * P:(m + 1) * P], ident_h[:])
                if kind == "I":
                    if t == 0:
                        pe.wait_ge(xq_ready, nth(half, 0, 1))
                    for k in range(2):
                        last = nc.tensor.transpose(bank16((kind, t), s0, BF16)[0:KC, k * P:(k + 1) * P],
                                                   xq[:, t, k * KC:(k + 1) * KC], ident_b[:])
                if kind == "X":
                    if t == 0:
                        pe.wait_ge(job_out["I"], nth(half, TH - 1, TH))
                    for k in range(2):
                        last = mm(ps, w1T[:, k, t * P:(t + 1) * P], xqT[:, k], start=(k == 0), stop=(k == 1))
                if kind == "W":
                    pe.wait_ge(ffn_quantised, 1 + t // 3)
                    for n in range(4):
                        if t < 3:
                            k, j = n // 2, 2 * t + n % 2
                            last = nc.tensor.transpose(ps[0:KC, n * P:(n + 1) * P], w1_nat[:, j, k * KC:(k + 1) * KC], ident[:])
                        else:
                            j, r = 2 * (t - 3) + n // 2, n % 2
                            last = nc.tensor.transpose(ps[:, n * KC:(n + 1) * KC], w2_nat[:, r, j::HB], ident[0:KC, 0:KC])
                if kind == "Y":
                    if t == 0:
                        pe.wait_ge(hq_ready, nth(half, HB - 1, HB))
                    for j in range(HB):
                        last = mm(ps[:, 0:C], hq[:, j, t * P:(t + 1) * P], w2T[:, j], start=(j == 0), stop=(j == HB - 1))
                last.then_inc(job_mm[kind], 1)

            def one(s0, s, b):
                for u in range(UNITS):
                    first, second = UNIT_WORK[u]
                    if attends(s0):
                        scores(s0, s, u)
                    for kind, t in first:
                        if kind in job_mm:
                            job(s0, s, kind, t)
                    if u and attends(s0):
                        heads(s0, s, u - 1)
                    elif not u and attends(s0 - 1):
                        heads(s0 - 1, s - 1, UNITS - 1)
                    for kind, t in second:
                        if kind in job_mm:
                            job(s0, s, kind, t)

            start()
            for kind, t, s in FIRST_WORK:
                if kind in JOB_KINDS:
                    job(s, s, kind, t)
            halfsteps(pe, one)


LINKS_PER_TURN = 4 * 62


_INS = ['x', 'mask_BS_i2_0', 'L0_tok_token_table', 'L0_tok_segm_table', 'L0_attn_qkv_weight',
        'L0_attn_proj_weight', 'L0_ffn_w1', 'L0_ffn_b1', 'L0_ffn_alpha_w1', 'L0_ffn_alpha_a1',
        'L0_ffn_w2', 'L0_ffn_b2', 'L0_ffn_alpha_w2', 'L0_ffn_alpha_a2']


def positions():
    import numpy as np
    at = np.arange(SEQ, dtype=np.float32)[:, None]
    ids = np.arange(C, dtype=np.float32)[None, :]
    even_exp = np.floor(ids / np.float32(2.0)) * np.float32(2.0) / np.float32(C)
    angle = at / np.power(np.float32(10000.0), even_exp)
    return np.where(np.arange(C) % 2 == 0, np.sin(angle), np.cos(angle)).astype(np.float32)


def kernel(**inputs):
    import numpy as np
    import concourse.bacc as bacc
    from concourse.bass_utils import run_bass_kernel_spmd

    nc = bacc.Bacc("TRN2", target_bir_lowering=False, num_devices=1)
    arrays, args = {}, []
    for name, a in [(n, inputs[n]) for n in _INS] + [("positions", positions())]:
        a = np.ascontiguousarray(a)
        arrays[f"in_{name}"] = a
        args.append(nc.dram_tensor(f"in_{name}", a.shape, mybir.dt.from_np(a.dtype), kind="ExternalInput").ap())
    out = nc.dram_tensor("out", (B, SEQ, C), F32, kind="ExternalOutput").ap()
    layer(nc, *args, out)
    r = run_bass_kernel_spmd(nc, [arrays], core_ids=[0])
    return r.results[0]["out"]
```
